# Optimizing a Trainium2 kernel written in Bass

```python
import numpy as np
import jax
import jax.numpy as jnp

def _softmax(x, axis=-1):
    return jax.nn.softmax(x, axis=axis)

def _gelu(x):
    return jax.nn.gelu(x, approximate=True)

def _silu(x):
    return jax.nn.silu(x)

def _sigmoid(x):
    return jax.nn.sigmoid(x)

def _layernorm(x, axis=-1, eps=1e-05):
    m = jnp.mean(x, axis=axis, keepdims=True)
    v = jnp.var(x, axis=axis, keepdims=True)
    return (x - m) / jnp.sqrt(v + eps)

def _scatter_add(tgt, idx, src, axis=0):
    return tgt.at[idx].add(src)

def _segment_sum(src, seg, n):
    return jax.ops.segment_sum(src, seg, n)
kernel_name = 'mk_adaln_d1_jaxref_r8_aaa1b8'

def setup_inputs(seed: int=0):
    np.random.seed(seed)
    _w = jnp.asarray

    def _L0_attn_setup():
        import math
        import jax, jax.numpy as jnp
        import numpy as np
        B, S, D, H, DH = (2, 256, 256, 16, 128)

        def _alibi_slopes(n):

            def pow2(m):
                start = 2 ** (-2 ** (-(math.log2(m) - 3)))
                return [start * start ** i for i in range(m)]
            if math.log2(n).is_integer():
                return pow2(n)
            c = 2 ** math.floor(math.log2(n))
            return pow2(c) + _alibi_slopes(2 * c)[0::2][:n - c]

        def _alibi_mask(n_heads, q_len, kv_len):
            slopes = jnp.asarray(np.array(_alibi_slopes(n_heads), dtype=np.float32))
            bias = slopes[:, None, None] * jnp.arange(kv_len, dtype=jnp.float32)[None, None, :]
            i = jnp.arange(q_len)[:, None]
            j = jnp.arange(kv_len)[None, :]
            causal = jnp.where(j > i, -jnp.inf, 0.0).astype(jnp.float32)
            return causal[None, :, :] + bias
        key = jax.random.key(seed)
        k1, k2, k3, k4, k5 = jax.random.split(key, 5)
        scale = 1.0 / math.sqrt(D)
        return {'resid_pre': jax.random.normal(k1, (B, S, D), dtype=jnp.float32), 'Wq': jax.random.normal(k2, (H * DH, D), dtype=jnp.float32) * scale, 'Wk': jax.random.normal(k3, (H * DH, D), dtype=jnp.float32) * scale, 'Wv': jax.random.normal(k4, (H * DH, D), dtype=jnp.float32) * scale, 'Wo': jax.random.normal(k5, (D, H * DH), dtype=jnp.float32) * scale}
    _L0_attn_in = _L0_attn_setup()

    def _L0_ffn_setup():
        import jax, jax.numpy as jnp
        import numpy as np

        def _sparsify_2to4(h):
            B, S, I = h.shape
            g = h.reshape(B, S, I // 4, 4)
            a = jnp.abs(g)
            _, idx = jax.lax.top_k(a, 2)
            pos = jnp.arange(4)
            mask = (pos == idx[..., 0:1]) | (pos == idx[..., 1:2])
            return (g * mask.astype(g.dtype)).reshape(B, S, I)
        key = jax.random.key(seed)
        k1, k2, k3, k4 = jax.random.split(key, 4)
        B, S, H, I = (4, 256, 256, 1024)
        x = jax.random.normal(k1, (B, S, H), dtype=jnp.float32)
        w_gate = jax.random.normal(k2, (H, I), dtype=jnp.float32) / np.sqrt(H)
        w_up = jax.random.normal(k3, (H, I), dtype=jnp.float32) / np.sqrt(H)
        w_down = jax.random.normal(k4, (I, H), dtype=jnp.float32) / np.sqrt(I)
        return {'x': x, 'w_gate': w_gate, 'w_up': w_up, 'w_down': w_down}
    _L0_ffn_in = _L0_ffn_setup()
    _L0_c = _w((lambda *s: np.random.randn(*s).astype(np.float32) * 0.05)(8, 256))
    _L0_wmod = _w((lambda *s: np.random.randn(*s).astype(np.float32) * 0.05)(256, 6 * 256) * 256 ** (-0.5))
    _d = {'L0_attn_resid_pre': _L0_attn_in['resid_pre'], 'L0_attn_Wq': _L0_attn_in['Wq'], 'L0_attn_Wk': _L0_attn_in['Wk'], 'L0_attn_Wv': _L0_attn_in['Wv'], 'L0_attn_Wo': _L0_attn_in['Wo'], 'L0_ffn_w_gate': _L0_ffn_in['w_gate'], 'L0_ffn_w_up': _L0_ffn_in['w_up'], 'L0_ffn_w_down': _L0_ffn_in['w_down'], 'L0_c': _L0_c, 'L0_wmod': _L0_wmod}
    _x0 = _d['L0_attn_resid_pre']
    _d['L0_attn_resid_pre'] = jax.random.normal(jax.random.fold_in(jax.random.key(seed), 1), (8, 512, 256), dtype=_x0.dtype)
    del _x0
    return _d

def reference(L0_attn_resid_pre, L0_attn_Wq, L0_attn_Wk, L0_attn_Wv, L0_attn_Wo, L0_ffn_w_gate, L0_ffn_w_up, L0_ffn_w_down, L0_c, L0_wmod):

    def _L0_attn_ref(resid_pre, Wq, Wk, Wv, Wo):
        import math
        import jax, jax.numpy as jnp
        import numpy as np
        B, S, D, H, DH = (2, 256, 256, 16, 128)

        def _alibi_slopes(n):

            def pow2(m):
                start = 2 ** (-2 ** (-(math.log2(m) - 3)))
                return [start * start ** i for i in range(m)]
            if math.log2(n).is_integer():
                return pow2(n)
            c = 2 ** math.floor(math.log2(n))
            return pow2(c) + _alibi_slopes(2 * c)[0::2][:n - c]

        def _alibi_mask(n_heads, q_len, kv_len):
            slopes = jnp.asarray(np.array(_alibi_slopes(n_heads), dtype=np.float32))
            bias = slopes[:, None, None] * jnp.arange(kv_len, dtype=jnp.float32)[None, None, :]
            i = jnp.arange(q_len)[:, None]
            j = jnp.arange(kv_len)[None, :]
            causal = jnp.where(j > i, -jnp.inf, 0.0).astype(jnp.float32)
            return causal[None, :, :] + bias
        b, s, d = resid_pre.shape
        q = (resid_pre @ Wq.T).reshape(b, s, H, DH)
        k = (resid_pre @ Wk.T).reshape(b, s, H, DH)
        v = (resid_pre @ Wv.T).reshape(b, s, H, DH)
        scores = jnp.einsum('bqhd,bkhd->bhqk', q, k) / math.sqrt(DH)
        scores = jnp.clip(scores, -1024.0, 1024.0)
        scores = scores + _alibi_mask(H, s, s)[None]
        attn = jax.nn.softmax(scores.astype(jnp.float32), axis=-1).astype(q.dtype)
        z = jnp.einsum('bhqk,bkhd->bqhd', attn, v)
        out = jnp.einsum('bqhd,ohd->bqo', z, Wo.reshape(d, H, DH))
        return out

    def _L0_ffn_ref(x, w_gate, w_up, w_down):
        import jax, jax.numpy as jnp
        import numpy as np

        def _sparsify_2to4(h):
            B, S, I = h.shape
            g = h.reshape(B, S, I // 4, 4)
            a = jnp.abs(g)
            _, idx = jax.lax.top_k(a, 2)
            pos = jnp.arange(4)
            mask = (pos == idx[..., 0:1]) | (pos == idx[..., 1:2])
            return (g * mask.astype(g.dtype)).reshape(B, S, I)
        h = jax.nn.silu(jnp.einsum('bsh,hi->bsi', x, w_gate)) * jnp.einsum('bsh,hi->bsi', x, w_up)
        h_sparse = _sparsify_2to4(h)
        return jnp.einsum('bsi,ih->bsh', h_sparse, w_down)
    x = L0_attn_resid_pre
    mod = (_silu(L0_c) @ L0_wmod).reshape(L0_c.shape[0], 6, 1, -1)
    sa, ca, ga, sb, cb, gb = (mod[:, 0], mod[:, 1], mod[:, 2], mod[:, 3], mod[:, 4], mod[:, 5])
    ga = (2 * (ga >= 0) - 1) * jnp.maximum(jnp.abs(ga), 0.25)
    gb = (2 * (gb >= 0) - 1) * jnp.maximum(jnp.abs(gb), 0.25)
    h = _layernorm(x, axis=-1) * (1 + ca) + sa
    x = x + ga * _L0_attn_ref(h, L0_attn_Wq, L0_attn_Wk, L0_attn_Wv, L0_attn_Wo)
    h = _layernorm(x, axis=-1) * (1 + cb) + sb
    x = x + gb * _L0_ffn_ref(h, L0_ffn_w_gate, L0_ffn_w_up, L0_ffn_w_down)
    return x

_drawn_inputs = setup_inputs


def setup_inputs(seed=0):
    import zlib

    import numpy as np

    out = dict(_drawn_inputs(seed))
    spreads = {}
    factors = {}
    for name, (base, spread) in spreads.items():
        noise = np.random.default_rng([zlib.crc32(name.encode()), seed]).standard_normal(out[name].shape)
        drawn = base * np.exp(spread * noise) if base else spread * noise
        out[name] = jnp.asarray(drawn.astype(out[name].dtype))
    for name, factor in factors.items():
        out[name] = (out[name] * factor).astype(out[name].dtype)
    return out
```

```python
import math
from contextlib import ExitStack

import numpy as np

import concourse.bass as bass
from concourse import mybir

F32 = mybir.dt.float32
F32R = mybir.dt.float32r
BF16 = mybir.dt.bfloat16
ACT = mybir.ActivationFunctionType
ALU = mybir.AluOpType

P = 128
B, S, D = 8, 512, 256
H, DH = 16, 128
HD = H * DH
I = 1024
KT = D // P
TT = S // P
GROUP = 4
CT = I // P // GROUP
LN_EPS = 1e-5
CLIP = 1024.0
MASKED = -1e30
SA, CA, GA, SB, CB, GB = range(6)

SLOPE = [float(np.float32((2 ** (-2 ** (-(math.log2(H) - 3)))) ** (h + 1))) for h in range(H)]

AREA = {3: 0, 2: 512, 0: 896, 1: 1024}
BANKS = [[3], [2, 0], [1]]
BANK_COLS = [(0, 512), (512, 1024), (1024, 1280)]
BLOCK_ORDER = [3, 2, 0, 1]
WIDTH = {i: P * (i + 1) for i in range(TT)}
KEY_AREA = {j: AREA[TT - 1 - j] for j in range(TT)}
KEY_BANKS = [[TT - 1 - i for i in blocks] for blocks in BANKS]
TRI = 1280


def wait_alone(eng, semaphore, value):
    eng.wait_ge(semaphore, value)
    eng.nop(nofuse=True)


def split_passes(hi_l, lo_l, hi_r, lo_r):
    return [(hi_l, hi_r), (hi_l, lo_r), (lo_l, hi_r)]


RING = 6
RING_PROLOGUE = 2 + 2 + 2


def ring_uses():
    uses = []
    for h in range(H):
        uses += [("s", h, n) for n in range(3)]
        if h >= 1:
            uses.append(("z", h - 1))
        if h < H - 1:
            uses += [("q", h + 1), ("k", h + 1)]
        else:
            uses += [("ln", 0), ("ln", 1)]
        uses += [("t", h, n) for n in range(3)]
        if h < H - 2:
            uses.append(("v", h))
    return uses + [("q", 0), ("k", 0), ("z", H - 1), ("v", H - 2), ("v", H - 1)]


USES = ring_uses()
PER_BATCH = len(USES)
assert PER_BATCH % RING == 0 and RING_PROLOGUE % RING == 0
USE = {u: n for n, u in enumerate(USES)}


def attention_phase(nc, x, cT, wmod, wqT, wkT, wvT, woT, attn_T, mods):
    with ExitStack() as ctx:
        def sb(name, shape, dt):
            return ctx.enter_context(nc.sbuf_tensor(name, shape, dt))

        def sem(name):
            return ctx.enter_context(nc.semaphore(name))

        wq = [sb(f"wq_{s}", [P, KT, HD], F32R) for s in ("hi", "lo")]
        wk = [sb(f"wk_{s}", [P, KT, HD], F32R) for s in ("hi", "lo")]
        wv = [sb(f"wv_{s}", [P, KT, HD], F32R) for s in ("hi", "lo")]
        wo = [sb(f"wo_{s}", [P, H, D], F32R) for s in ("hi", "lo")]
        hT = [sb(f"hT_{s}", [P, KT, S], F32R) for s in ("hi", "lo")]
        qT = [sb(f"qT_{s}", [P, S], F32R) for s in ("hi", "lo")]
        kT = [sb(f"kT_{s}", [P, S], F32R) for s in ("hi", "lo")]
        zT = [sb(f"zT_{s}", [P, S], F32R) for s in ("hi", "lo")]
        v = [sb(f"v_{s}", [P, 2, TT, 2 * DH], F32R) for s in ("hi", "lo")]
        pT = [sb(f"pT_{s}", [P, TRI], F32R) for s in ("hi", "lo")]
        probs = sb("probs", [P, TRI], F32)
        key_pos = sb("key_pos", [P, TRI], F32)
        xin = sb("xin", [P, TT, D], F32)
        h_full = sb("h_full", [P, KT, S], F32)
        out_T = sb("out_T", [P, KT, S], F32)
        ident = sb("ident", [P, P], F32)
        stage = [sb(f"stage{i}", [P, 1024], F32) for i in range(2)]
        c_sb = sb("c_sb", [P, KT, B], F32)
        c_exp = sb("c_exp", [P, KT, B], F32)
        c_silu = sb("c_silu", [P, KT, B], F32)
        mod_sign = sb("mod_sign", [P, 2, B], F32)
        mod_abs = sb("mod_abs", [P, 2, B], F32)
        mod_ln = sb("mod_ln", [P, 4], F32)
        gate_now = sb("gate_now", [P, KT], F32)
        neg_max = sb("neg_max", [P, TT], F32)
        row_sum = sb("row_sum", [P, TT], F32)
        row_inv = sb("row_inv", [P, TT], F32)
        bn = sb("bn", [P, TT, 6], F32)
        mv = sb("mv", [P, TT, 2], F32)
        var_eps = sb("var_eps", [P, TT], F32)
        minus_half = sb("minus_half", [P, TT], F32)
        rstd = sb("rstd", [P, TT], F32)
        neg_mean = sb("neg_mean", [P, TT], F32)
        shift = sb("shift", [P, TT], F32)

        out_ps = [ctx.enter_context(nc.psum_tensor(f"out_ps{i}", [P, S], F32)) for i in range(KT)]
        ring = [ctx.enter_context(nc.psum_tensor(f"ring{i}", [P, 512], F32)) for i in range(RING)]

        staged = [sem(f"staged{i}") for i in range(2)]
        c_loaded = sem("c_loaded")
        stage_hi = sem("stage_hi")
        stage_free = sem("stage_free")
        c_exp_done = sem("c_exp_done")
        c_steps = sem("c_steps")
        c_ready = sem("c_ready")
        mods_steps = sem("mods_steps")
        constants = sem("constants")
        x_loaded = sem("x_loaded")
        stats_steps = sem("stats_steps")
        stats_ready = sem("stats_ready")
        norm_steps = sem("norm_steps")
        x_normed = sem("x_normed")
        mod_picked = sem("mod_picked")
        hT_hi = sem("hT_hi")
        hT_ready = sem("hT_ready")
        ring_filled = sem("ring_filled")
        ring_hi = sem("ring_hi")
        ring_freed = sem("ring_freed")
        max_ready = sem("max_ready")
        exp_done = sem("exp_done")
        inv_ready = sem("inv_ready")
        probs_ready = sem("probs_ready")
        out_summed = sem("out_summed")
        gate_picked = sem("gate_picked")
        out_taken = sem("out_taken")
        out_T_free = sem("out_T_free")

        MOD_CHUNKS = 3
        weights = [(wqT, wq), (wkT, wk), (wvT, wv), (woT, wo)]
        W_CHUNKS = 4
        CHUNKS = MOD_CHUNKS + W_CHUNKS * len(weights)

        def weight_chunk(n, s):
            w, c = divmod(n - MOD_CHUNKS, W_CHUNKS)
            return weights[w][1][s][:, :, :].rearrange("p a n -> p (a n)")[:, c * 1024:(c + 1) * 1024]

        def ring_no(b, use):
            return RING_PROLOGUE + b * PER_BATCH + use

        def ring_as(use, like):
            bank = ring[use % RING]
            return bank[:, :].rearrange("p (t n) -> p t n", t=2) if len(like.shape) == 3 else bank[:, 0:like.shape[1]]

        def slope_scale(h):
            return 1.0 / (math.sqrt(DH) * SLOPE[h])

        block = ctx.enter_context(nc.Block())

        @block.sync
        def _(sp):
            sp.dma_start(c_sb[:, :, :], cT).then_inc(c_loaded, 16)
            sp.dma_start(xin[:, :, :], x[0].rearrange("(t p) d -> p t d", p=P)).then_inc(x_loaded, 16)
            for n in range(CHUNKS):
                if n >= 2:
                    sp.wait_ge(stage_free, n - 1)
                if n < MOD_CHUNKS:
                    sp.dma_start(stage[n % 2][:, :].rearrange("p (k n) -> p k n", k=KT),
                                 wmod[:, :, n * 512:(n + 1) * 512]).then_inc(staged[n % 2], 16)
                else:
                    w, c = divmod(n - MOD_CHUNKS, W_CHUNKS)
                    sp.dma_start(stage[n % 2][:, :], weights[w][0][:, c * 1024:(c + 1) * 1024]).then_inc(staged[n % 2], 16)

            def step(b, load):
                if load:
                    sp.wait_ge(hT_ready, 2 * b + 2)
                    sp.dma_start(xin[:, :, :],
                                 x[bass.ds(b + 1, 1)].rearrange("o (t p) d -> p (o t) d", p=P)).then_inc(x_loaded, 16)
                sp.wait_ge(out_taken, KT * (b + 2))
                sp.dma_start(attn_T[bass.ds(b, 1)].rearrange("o (k p) n -> p (o k) n", p=P),
                             out_T[:, :, :]).then_inc(out_T_free, 16)

            with sp.Fori(0, B - 1) as b:
                step(b, True)
            sp.wait_ge(hT_ready, 2 * B)
            sp.dma_start(xin[:, :, :], x[0].rearrange("(t p) d -> p t d", p=P)).then_inc(x_loaded, 16)
            sp.wait_ge(out_taken, KT * (B + 1))
            sp.dma_start(attn_T[B - 1].rearrange("(k p) n -> p k n", p=P), out_T[:, :, :]).then_inc(out_T_free, 16)
            sp.wait_ge(out_T_free, 16 * (B + 1))

        @block.gpsimd
        def _(pool):
            pool.memset(out_T[:, 0, 0:1], 0.0).then_inc(out_T_free, 16)
            pool.memset(minus_half[:, :], -0.5).then_inc(constants, 1)
            pool.memset(mods[:, :, :], 0.0).then_inc(constants, 1)
            pool.memset(ident[:, :], 0.0).then_inc(constants, 1)
            pool.iota(key_pos[:, 0:512], pattern=[[1, 512]], base=0, channel_multiplier=0,
                      allow_small_or_imprecise_dtypes=True).then_inc(constants, 1)
            pool.wait_ge(constants, 4)
            pool.affine_select(out=ident[:, :], in_=ident[:, :], compare_op=ALU.not_equal, fill=1.0, base=0,
                               pattern=[[-1, P]], channel_multiplier=1).then_inc(constants, 1)
            for i in range(TT - 1):
                pool.tensor_copy(key_pos[:, AREA[i]:AREA[i] + WIDTH[i]], key_pos[:, 0:WIDTH[i]]).then_inc(constants, 1)
            pool.wait_ge(constants, 8)
            for i in range(TT):
                diag = key_pos[:, AREA[i] + P * i:AREA[i] + P * (i + 1)]
                pool.affine_select(out=diag, in_=diag, compare_op=ALU.is_ge, fill=MASKED, base=0,
                                   pattern=[[-1, P]], channel_multiplier=1).then_inc(constants, 1)

            def layernorm(count):
                wait_alone(pool, stats_ready, count)
                pool.tensor_scalar(var_eps[:, :], mv[:, :, 1], LN_EPS, 1.0, ALU.add, ALU.mult).then_inc(norm_steps, 1)
                pool.tensor_scalar(neg_mean[:, :], mv[:, :, 0], -1.0, 1.0, ALU.mult, ALU.mult).then_inc(norm_steps, 1)
                pool.wait_ge(norm_steps, 4 * count - 2)
                pool.tensor_tensor(rstd[:, :], var_eps[:, :], minus_half[:, :], ALU.pow).then_inc(norm_steps, 1)
                pool.wait_ge(norm_steps, 4 * count - 1)
                pool.tensor_tensor(shift[:, :], neg_mean[:, :], rstd[:, :], ALU.mult).then_inc(norm_steps, 1)
                wait_alone(pool, norm_steps, 4 * count)
                for t in range(TT):
                    pool.tensor_scalar(xin[:, t, :], xin[:, t, :], rstd[:, t:t + 1], shift[:, t:t + 1],
                                       ALU.mult, ALU.add).then_inc(x_normed, 1)

            layernorm(1)
            with pool.Fori(0, B) as b:
                for h in range(H):
                    for n, i in enumerate(BLOCK_ORDER):
                        if n in (0, 3):
                            wait_alone(pool, inv_ready, (b * H + h) * 2 + (1 if n == 0 else 2))
                        blk = probs[:, AREA[i]:AREA[i] + WIDTH[i]]
                        pool.tensor_scalar(blk, blk, row_inv[:, n:n + 1], 1.0, ALU.mult, ALU.mult).then_inc(probs_ready, 1)
                    if h == 7:
                        layernorm(b + 2)

        @block.scalar
        def _(act):
            act.wait_ge(c_loaded, 16)
            act.activation(c_exp[:, :, :], c_sb[:, :, :], ACT.Exp, scale=-1.0).then_inc(c_exp_done, 1)

            for n in range(MOD_CHUNKS, CHUNKS):
                act.wait_ge(staged[n % 2], 16 * (n // 2 + 1))
                act.copy(weight_chunk(n, 0), stage[n % 2][:, :]).then_inc(stage_hi, 1)

            def hi(use_static, use_count, dst, scale=1.0):
                act.wait_ge(ring_filled, use_count + 1)
                act.activation(dst, ring_as(use_static, dst), ACT.Copy, scale=scale).then_inc(ring_hi, 1)

            def h_hi(count, uses):
                for k in range(KT):
                    act.wait_ge(ring_freed, uses[k] + 1)
                    act.copy(hT[0][:, k, :], h_full[:, k, :]).then_inc(hT_hi, 1)

            h_hi(1, [0, 1])
            hi(2, 2, qT[0][:, :], slope_scale(0))
            hi(3, 3, kT[0][:, :])
            hi(4, 4, v[0][:, 0, 0:2, :])
            hi(5, 5, v[0][:, 0, 2:4, :])

            with act.Fori(0, B) as b:
                act.wait_ge(out_taken, KT * (b + 1))
                act.copy(gate_now[:, :], mods[:, 2 * GA:2 * GA + 2, bass.ds(b, 1)]
                         .rearrange("p m o -> p (m o)")).then_inc(gate_picked, 1)

                def ring_hi_of(key, dst, scale=1.0):
                    hi(RING_PROLOGUE + USE[key], ring_no(b, USE[key]), dst, scale)

                def probs_hi(h):
                    for n, (lo, up) in enumerate(BANK_COLS):
                        ring_hi_of(("t", h, n), pT[0][:, lo:up])

                for h in range(H):
                    for n, i in enumerate(BLOCK_ORDER):
                        blk = probs[:, AREA[i]:AREA[i] + WIDTH[i]]
                        act.wait_ge(max_ready, (b * H + h) * TT + n + 1)
                        act.activation(blk, blk, ACT.Exp, bias=neg_max[:, i:i + 1], scale=-1.0,
                                       accum_out=row_sum[:, n:n + 1]).then_inc(exp_done, 1)
                        if h >= 1 and n == 2:
                            ring_hi_of(("z", h - 1), zT[0][:, :])
                    if h < H - 1:
                        ring_hi_of(("q", h + 1), qT[0][:, :], slope_scale(h + 1))
                        ring_hi_of(("k", h + 1), kT[0][:, :])
                        probs_hi(h)
                        if h < H - 2:
                            pair, half = (h // 2 + 1) % 2, 2 * (h % 2)
                            ring_hi_of(("v", h), v[0][:, pair, half:half + 2, :])
                    else:
                        h_hi(b + 2, [ring_no(b, USE[("ln", k)]) for k in range(KT)])
                        probs_hi(h)
                        ring_hi_of(("q", 0), qT[0][:, :], slope_scale(0))
                        ring_hi_of(("k", 0), kT[0][:, :])
                        ring_hi_of(("z", H - 1), zT[0][:, :])
                        ring_hi_of(("v", H - 2), v[0][:, 0, 0:2, :])
                        ring_hi_of(("v", H - 1), v[0][:, 0, 2:4, :])
                act.wait_ge(out_summed, b + 1)
                act.wait_ge(out_T_free, 16 * b + 16)
                act.wait_ge(gate_picked, b + 1)
                act.activation(out_T[:, 0, :], out_ps[0][:, :], ACT.Copy, scale=gate_now[:, 0:1]).then_inc(out_taken, 1)
                act.activation(out_T[:, 1, :], out_ps[1][:, :], ACT.Copy, scale=gate_now[:, 1:2]).then_inc(out_taken, 1)

        @block.vector
        def _(dve):
            dve.wait_ge(c_exp_done, 1)
            dve.tensor_scalar(c_exp[:, :, :], c_exp[:, :, :], 1.0, None, ALU.add).then_inc(c_steps, 1)
            dve.wait_ge(c_steps, 1)
            dve.reciprocal(c_exp[:, :, :], c_exp[:, :, :]).then_inc(c_steps, 1)
            dve.wait_ge(c_steps, 2)
            dve.tensor_tensor(c_silu[:, :, :], c_sb[:, :, :], c_exp[:, :, :], ALU.mult).then_inc(c_ready, 1)
            dve.wait_ge(stage_free, MOD_CHUNKS)
            dve.wait_ge(constants, 4)
            dve.tensor_copy(mods[:, :, 0:B], out_ps[0][:, 0:12 * B].rearrange("p (m b) -> p m b", b=B)).then_inc(out_taken, KT)
            dve.wait_ge(out_taken, KT)
            for k in (CA, CB):
                m = mods[:, 2 * k:2 * k + 2, 0:B]
                dve.tensor_scalar(m, m, 1.0, None, ALU.add).then_inc(mods_steps, 1)
            for n, k in enumerate((GA, GB)):
                m = mods[:, 2 * k:2 * k + 2, 0:B]
                dve.tensor_scalar(mod_sign[:, :, :], m, 0.0, 2.0, ALU.is_ge, ALU.mult).then_inc(mods_steps, 1)
                dve.scalar_tensor_tensor(out=mod_abs[:, :, :], in0=m, scalar=-1.0, in1=m, op0=ALU.mult,
                                         op1=ALU.max).then_inc(mods_steps, 1)
                dve.wait_ge(mods_steps, 4 + 4 * n)
                dve.tensor_scalar(mod_abs[:, :, :], mod_abs[:, :, :], 0.25, None, ALU.max).then_inc(mods_steps, 1)
                dve.wait_ge(mods_steps, 5 + 4 * n)
                dve.scalar_tensor_tensor(out=m, in0=mod_sign[:, :, :], scalar=-1.0, in1=mod_abs[:, :, :],
                                         op0=ALU.add, op1=ALU.mult).then_inc(mods_steps, 1)
                dve.wait_ge(mods_steps, 6 + 4 * n)

            for n in range(MOD_CHUNKS, CHUNKS):
                dve.wait_ge(stage_hi, n - MOD_CHUNKS + 1)
                dve.tensor_tensor(weight_chunk(n, 1), stage[n % 2][:, :], weight_chunk(n, 0).bitcast(F32),
                                  ALU.subtract).then_inc(stage_free, 1)

            def statistics(count, tiles=range(TT)):
                if tiles[0] == 0:
                    dve.wait_ge(x_loaded, 16 * count)
                for t in tiles:
                    dve.bn_stats(bn[:, t, :], xin[:, t, :]).then_inc(stats_steps, 1)
                if tiles[-1] == TT - 1:
                    wait_alone(dve, stats_steps, TT * count)
                    for t in range(TT):
                        last = dve.bn_aggr(mv[:, t, :], bn[:, t, :])
                    last.then_inc(stats_ready, 1)

            def modulate(uses, counts, batch, count):
                dve.tensor_copy(mod_ln[:, 0:2], mods[:, 2 * CA:2 * CA + 2, batch].rearrange("p m o -> p (m o)"))\
                   .then_inc(mod_picked, 1)
                dve.tensor_copy(mod_ln[:, 2:4], mods[:, 2 * SA:2 * SA + 2, batch].rearrange("p m o -> p (m o)"))\
                   .then_inc(mod_picked, 1)
                dve.wait_ge(mod_picked, 2 * count)
                for k in range(KT):
                    dve.wait_ge(ring_filled, counts[k] + 1)
                    dve.tensor_scalar(h_full[:, k, :], ring[uses[k] % RING][:, :], mod_ln[:, k:k + 1],
                                      mod_ln[:, 2 + k:3 + k], ALU.mult, ALU.add).then_inc(ring_freed, 1)
                for k in range(KT):
                    dve.wait_ge(hT_hi, KT * (count - 1) + k + 1)
                    dve.tensor_tensor(hT[1][:, k, :], h_full[:, k, :], hT[0][:, k, :].bitcast(F32),
                                      ALU.subtract).then_inc(hT_ready, 1)

            def lo(use, count_hi, parts, scale=None):
                dve.wait_ge(ring_hi, count_hi)
                if scale is None:
                    dve.tensor_tensor(parts[1], ring_as(use, parts[1]), parts[0].bitcast(F32),
                                      ALU.subtract).then_inc(ring_freed, 1)
                else:
                    dve.scalar_tensor_tensor(out=parts[1], in0=ring_as(use, parts[1]), scalar=scale,
                                             in1=parts[0].bitcast(F32), op0=ALU.mult,
                                             op1=ALU.subtract).then_inc(ring_freed, 1)

            statistics(1)
            modulate([0, 1], [0, 1], slice(0, 1), 1)
            lo(2, 1, [t[:, :] for t in qT], slope_scale(0))
            lo(3, 2, [t[:, :] for t in kT])
            lo(4, 3, [t[:, 0, 0:2, :] for t in v])
            lo(5, 4, [t[:, 0, 2:4, :] for t in v])
            split_uses = [u for u in USES if u[0] not in ("ln", "s")]
            HI_PROLOGUE, HI_BATCH = 4, len(split_uses)
            HI = {u: n for n, u in enumerate(split_uses)}

            with dve.Fori(0, B) as b:
                def lo_of(key, parts, scale=None):
                    lo(RING_PROLOGUE + USE[key], HI_PROLOGUE + b * HI_BATCH + HI[key] + 1, parts, scale)

                def probs_lo(h):
                    for n, (a, z) in enumerate(BANK_COLS):
                        lo_of(("t", h, n), [t[:, a:z] for t in pT])

                dve.wait_ge(constants, 12)
                for h in range(H):
                    limit = CLIP / SLOPE[h]
                    for n, (a, z) in enumerate(BANK_COLS):
                        use = USE[("s", h, n)]
                        dve.wait_ge(ring_filled, ring_no(b, use) + 1)
                        dve.tensor_scalar(probs[:, a:z], ring[(RING_PROLOGUE + use) % RING][:, 0:z - a],
                                          limit, -limit, ALU.min, ALU.max).then_inc(ring_freed, 1)
                        wait_alone(dve, ring_freed, ring_no(b, use) + 1)
                        for i in BANKS[n]:
                            blk = probs[:, AREA[i]:AREA[i] + WIDTH[i]]
                            dve.tensor_tensor_reduce(blk, blk, key_pos[:, AREA[i]:AREA[i] + WIDTH[i]], -SLOPE[h], 3e38,
                                                     ALU.add, ALU.min, neg_max[:, i:i + 1]).then_inc(max_ready, 1)
                    dve.wait_ge(exp_done, (b * H + h) * TT + 3)
                    dve.reciprocal(row_inv[:, 0:3], row_sum[:, 0:3]).then_inc(inv_ready, 1)
                    if h >= 1:
                        lo_of(("z", h - 1), [t[:, :] for t in zT])
                    dve.wait_ge(exp_done, (b * H + h + 1) * TT)
                    dve.reciprocal(row_inv[:, 3:4], row_sum[:, 3:4]).then_inc(inv_ready, 1)
                    if h < H - 1:
                        lo_of(("q", h + 1), [t[:, :] for t in qT], slope_scale(h + 1))
                        lo_of(("k", h + 1), [t[:, :] for t in kT])
                        probs_lo(h)
                        if h < H - 2:
                            pair, half = (h // 2 + 1) % 2, 2 * (h % 2)
                            lo_of(("v", h), [t[:, pair, half:half + 2, :] for t in v])
                        if 3 <= h < 3 + TT:
                            statistics(b + 2, [h - 3])
                    else:
                        modulate([RING_PROLOGUE + USE[("ln", k)] for k in range(KT)],
                                 [ring_no(b, USE[("ln", k)]) for k in range(KT)], bass.ds(b + 1, 1), b + 2)
                        probs_lo(h)
                        lo_of(("q", 0), [t[:, :] for t in qT], slope_scale(0))
                        lo_of(("k", 0), [t[:, :] for t in kT])
                        lo_of(("z", H - 1), [t[:, :] for t in zT])
                        lo_of(("v", H - 2), [t[:, 0, 0:2, :] for t in v])
                        lo_of(("v", H - 1), [t[:, 0, 2:4, :] for t in v])

        @block.tensor
        def _(pe):
            pe.wait_ge(constants, 5)
            for n in range(MOD_CHUNKS):
                pe.wait_ge(staged[n % 2], 16 * (n // 2 + 1))
                if n == 0:
                    pe.wait_ge(c_ready, 1)
                w = stage[n % 2][:, :].rearrange("p (k n) -> p k n", k=KT)
                for t in range(4):
                    m = 4 * n + t
                    for k in range(KT):
                        mm = pe.matmul(out_ps[0][:, m * B:(m + 1) * B], w[:, k, t * P:(t + 1) * P], c_silu[:, k, :],
                                       start=(k == 0), stop=(k == KT - 1))
                mm.then_inc(stage_free, 1)

            def accumulate(out, terms):
                for n, (l, r) in enumerate(terms):
                    mm = pe.matmul(out, l, r, start=(n == 0), stop=(n == len(terms) - 1))
                return mm

            def claim(count, static):
                if isinstance(count, int) and count < RING:
                    return ring[static % RING]
                pe.wait_ge(ring_freed, count - RING + 1)
                return ring[static % RING]

            def turn_x(statics, counts, ln_count):
                for k in range(KT):
                    bank = claim(counts[k], statics[k])
                    for t in range(TT):
                        if k == 0:
                            pe.wait_ge(x_normed, TT * (ln_count - 1) + t + 1)
                        mm = pe.transpose(bank[:, t * P:(t + 1) * P], xin[:, t, k * P:(k + 1) * P], ident[:, :])
                    mm.then_inc(ring_filled, 1)

            def project(static, count, w, h):
                bank = claim(count, static)
                cols = slice(h * DH, (h + 1) * DH)
                terms = []
                for k in range(KT):
                    terms += split_passes(w[0][:, k, cols], w[1][:, k, cols], hT[0][:, k, :], hT[1][:, k, :])
                accumulate(bank[:, :], terms).then_inc(ring_filled, 1)

            def project_v(static, count, pair, half):
                bank = claim(count, static)
                cols = slice(pair * 2 * DH, (pair + 1) * 2 * DH)
                for t in range(2):
                    rows = slice((half + t) * P, (half + t + 1) * P)
                    terms = []
                    for k in range(KT):
                        terms += split_passes(hT[0][:, k, rows], hT[1][:, k, rows], wv[0][:, k, cols], wv[1][:, k, cols])
                    mm = accumulate(bank[:, t * 256:(t + 1) * 256], terms)
                mm.then_inc(ring_filled, 1)

            turn_x([0, 1], [0, 1], 1)
            pe.wait_ge(stage_free, CHUNKS)
            pe.wait_ge(hT_ready, KT)
            project(2, 2, wq, 0)
            project(3, 3, wk, 0)
            project_v(4, 4, 0, 0)
            project_v(5, 5, 0, 2)

            with pe.Fori(0, B) as b:
                def at(key):
                    return RING_PROLOGUE + USE[key], ring_no(b, USE[key])

                def scores(h):
                    ready = USE[("k", h)] + 1 if h else USE[("k", 0)] - PER_BATCH + 2
                    pe.wait_ge(ring_freed, ring_no(b, ready))
                    for n, blocks in enumerate(BANKS):
                        static, count = at(("s", h, n))
                        bank = claim(count, static)
                        for i in blocks:
                            rows = slice(i * P, (i + 1) * P)
                            cols = slice(AREA[i] - BANK_COLS[n][0], AREA[i] - BANK_COLS[n][0] + WIDTH[i])
                            mm = accumulate(bank[:, cols], split_passes(qT[0][:, rows], qT[1][:, rows],
                                                                        kT[0][:, 0:WIDTH[i]], kT[1][:, 0:WIDTH[i]]))
                        mm.then_inc(ring_filled, 1)

                def turn_probs(h):
                    pe.wait_ge(probs_ready, (b * H + h) * TT + TT)
                    for n, keys in enumerate(KEY_BANKS):
                        static, count = at(("t", h, n))
                        bank = claim(count, static)
                        for j in keys:
                            for i in range(j, TT):
                                col = KEY_AREA[j] - BANK_COLS[n][0] + (i - j) * P
                                mm = pe.transpose(bank[:, col:col + P], probs[:, AREA[i] + j * P:AREA[i] + (j + 1) * P],
                                                  ident[:, :])
                        mm.then_inc(ring_filled, 1)

                def attend(h):
                    pe.wait_ge(ring_freed, ring_no(b, USE[("v", 2 * (h // 2) - 1)]) + 1 if h >= 2 else ring_no(b, 0))
                    static, count = at(("z", h))
                    bank = claim(count, static)
                    for m, keys in enumerate(KEY_BANKS):
                        pe.wait_ge(ring_freed, ring_no(b, USE[("t", h, m)]) + 1)
                        for j in keys:
                            cols = slice(KEY_AREA[j], KEY_AREA[j] + S - j * P)
                            vj = [t[:, (h // 2) % 2, j, (h % 2) * DH:(h % 2 + 1) * DH] for t in v]
                            for n, (l, r) in enumerate(split_passes(vj[0], vj[1], pT[0][:, cols], pT[1][:, cols])):
                                mm = pe.matmul(bank[:, j * P:S], l, r, start=(j == 0 and n == 0),
                                               stop=(j == KEY_BANKS[-1][-1] and n == 2))
                    mm.then_inc(ring_filled, 1)

                def project_out(h):
                    pe.wait_ge(ring_freed, ring_no(b, USE[("z", h)]) + 1)
                    if h == 0:
                        pe.wait_ge(out_taken, KT * (b + 1))
                    for k in range(KT):
                        cols = slice(k * P, (k + 1) * P)
                        terms = split_passes(wo[0][:, h, cols], wo[1][:, h, cols], zT[0][:, :], zT[1][:, :])
                        for n, (l, r) in enumerate(terms):
                            mm = pe.matmul(out_ps[k][:, :], l, r, start=(h == 0 and n == 0),
                                           stop=(h == H - 1 and n == 2))
                    if h == H - 1:
                        mm.then_inc(out_summed, 1)

                for h in range(H):
                    scores(h)
                    if h >= 1:
                        attend(h - 1)
                    if h < H - 1:
                        project(*at(("q", h + 1)), wq, h + 1)
                        project(*at(("k", h + 1)), wk, h + 1)
                        if h >= 1:
                            project_out(h - 1)
                        turn_probs(h)
                        if h < H - 2:
                            project_v(*at(("v", h)), (h // 2 + 1), 2 * (h % 2))
                    else:
                        turn_x([RING_PROLOGUE + USE[("ln", k)] for k in range(KT)],
                               [ring_no(b, USE[("ln", k)]) for k in range(KT)], b + 2)
                        project_out(h - 1)
                        turn_probs(h)
                        pe.wait_ge(hT_ready, KT * (b + 2))
                        project(*at(("q", 0)), wq, 0)
                        project(*at(("k", 0)), wk, 0)
                        attend(h)
                        project_v(*at(("v", H - 2)), 0, 0)
                        project_out(h)
                        project_v(*at(("v", H - 1)), 0, 2)


def mlp_phase(nc, x, attn_T, wg_in, wu_in, wd_in, out, mods):
    UNITS = CT * GROUP
    with ExitStack() as ctx:
        def sb(name, shape, dt):
            return ctx.enter_context(nc.sbuf_tensor(name, shape, dt))

        def sem(name):
            return ctx.enter_context(nc.semaphore(name))

        def ps(name):
            return ctx.enter_context(nc.psum_tensor(name, [P, 512], F32))

        wg = [sb(f"wg_{s}", [P, KT, I], F32R) for s in ("hi", "lo")]
        wu = [sb(f"wu_{s}", [P, KT, I], F32R) for s in ("hi", "lo")]
        wd = [sb(f"wd_{s}", [P, UNITS, D], F32R) for s in ("hi", "lo")]
        stage = [sb(f"mlp_stage{i}", [P, 1024], F32) for i in range(6)]
        x2 = sb("x2", [P, TT, D], F32)
        attn_in = sb("attn_in", [P, KT, S], F32)
        x1 = [sb(f"x1_{i}", [P, TT, D], F32) for i in range(2)]
        x1_hat = sb("x1_hat", [P, TT, D], F32)
        h2_full = sb("h2_full", [P, KT, S], F32)
        h2T = [sb(f"h2T_{s}", [P, KT, S], F32R) for s in ("hi", "lo")]
        silu = [sb(f"silu{i}", [P, S], F32) for i in range(2)]
        hid = [sb(f"hid{i}", [P, GROUP, S], F32) for i in range(2)]
        mag = sb("mag", [P, GROUP, S], F32)
        beats = sb("beats", [P, 6, S], BF16)
        wins = sb("wins", [P, GROUP, S], BF16)
        kept = [[sb(f"kept{c}_{s}", [P, GROUP, S], F32R) for s in ("hi", "lo")] for c in range(CT)]
        y_T = sb("y_T", [P, KT, S], F32)
        y_out = sb("y_out", [P, TT, D], F32)
        ident = sb("ident2", [P, P], F32)
        minus_half = sb("minus_half2", [P, TT], F32)
        mod_ln = sb("mod_ln2", [P, 4], F32)
        gate_now = sb("gate_now2", [P, KT], F32)
        bn = sb("bn2", [P, TT, 6], F32)
        mv = sb("mv2", [P, TT, 2], F32)
        var_eps = sb("var_eps2", [P, TT], F32)
        rstd = sb("rstd2", [P, TT], F32)
        neg_mean = sb("neg_mean2", [P, TT], F32)
        shift = sb("shift2", [P, TT], F32)

        gate_ps = [ps(f"gate_ps{i}") for i in range(2)]
        up_ps = [ps(f"up_ps{i}") for i in range(2)]
        down_ps = [ps(f"down_ps{i}") for i in range(KT)]
        turn_ps = [ps(f"turn_ps{i}") for i in range(KT)]

        staged = [sem(f"mlp_staged{i}") for i in range(6)]
        stage_hi = sem("mlp_stage_hi")
        weights_ready = sem("mlp_weights_ready")
        constants = sem("mlp_constants")
        x_loaded = sem("mlp_x_loaded")
        attn_loaded = sem("mlp_attn_loaded")
        turned = sem("mlp_turned")
        x1_ready = sem("mlp_x1_ready")
        stats_steps = sem("mlp_stats_steps")
        stats_ready = sem("mlp_stats_ready")
        norm_steps = sem("mlp_norm_steps")
        x1_normed = sem("mlp_x1_normed")
        mod_picked = sem("mlp_mod_picked")
        h2_full_ready = sem("mlp_h2_full_ready")
        h2_hi = sem("mlp_h2_hi")
        h2_ready = sem("mlp_h2_ready")
        unit_done = sem("mlp_unit_done")
        silu_done = sem("mlp_silu_done")
        hid_ready = sem("mlp_hid_ready")
        mag_ready = sem("mlp_mag_ready")
        rank_steps = sem("mlp_rank_steps")
        kept_full = sem("mlp_kept_full")
        kept_hi = sem("mlp_kept_hi")
        kept_ready = sem("mlp_kept_ready")
        down_summed = sem("mlp_down_summed")
        gate_picked = sem("mlp_gate_picked")
        y_scaled = sem("mlp_y_scaled")
        y_ready = sem("mlp_y_ready")
        stored = sem("mlp_stored")

        STAGES = 6
        loads = [(w_in, w, c) for w_in, w in ((wg_in, wg), (wu_in, wu), (wd_in, wd)) for c in range(2)]

        def part(n, s):
            _, w, c = loads[n]
            return w[s][:, :, :].rearrange("p a n -> p (a n)")[:, c * 1024:(c + 1) * 1024]

        block = ctx.enter_context(nc.Block())

        @block.sync
        def _(sp):
            sp.dma_start(x2[:, :, :], x[0].rearrange("(t p) d -> p t d", p=P)).then_inc(x_loaded, 16)
            sp.dma_start(attn_in[:, :, :], attn_T[0].rearrange("(k p) n -> p k n", p=P)).then_inc(attn_loaded, 16)
            for n, (w_in, _, c) in enumerate(loads):
                sp.dma_start(stage[n][:, :], w_in[:, c * 1024:(c + 1) * 1024]).then_inc(staged[n], 16)

            def load(b):
                sp.wait_ge(x1_ready, KT * b)
                sp.dma_start(x2[:, :, :], x[bass.ds(b, 1)].rearrange("o (t p) d -> p (o t) d", p=P)).then_inc(x_loaded, 16)
                sp.dma_start(attn_in[:, :, :], attn_T[bass.ds(b, 1)].rearrange("o (k p) n -> p (o k) n", p=P))\
                  .then_inc(attn_loaded, 16)

            def store(b):
                sp.wait_ge(y_ready, KT * (b + 1))
                sp.dma_start(out[bass.ds(b, 1)].rearrange("o (t p) d -> p (o t) d", p=P), y_out[:, :, :]).then_inc(stored, 16)

            load(1)
            with sp.Fori(2, B) as b:
                load(b)
                store(b - 2)
            store(B - 2)
            store(B - 1)
            sp.wait_ge(stored, 16 * B)

        @block.gpsimd
        def _(pool):
            pool.memset(minus_half[:, :], -0.5).then_inc(constants, 1)
            pool.memset(ident[:, :], 0.0).then_inc(constants, 1)
            pool.wait_ge(constants, 2)
            pool.affine_select(out=ident[:, :], in_=ident[:, :], compare_op=ALU.not_equal, fill=1.0, base=0,
                               pattern=[[-1, P]], channel_multiplier=1).then_inc(constants, 1)

            def layernorm(b):
                wait_alone(pool, stats_ready, b + 1)
                pool.tensor_scalar(var_eps[:, :], mv[:, :, 1], LN_EPS, 1.0, ALU.add, ALU.mult).then_inc(norm_steps, 1)
                pool.tensor_scalar(neg_mean[:, :], mv[:, :, 0], -1.0, 1.0, ALU.mult, ALU.mult).then_inc(norm_steps, 1)
                pool.wait_ge(norm_steps, 4 * b + 2)
                pool.tensor_tensor(rstd[:, :], var_eps[:, :], minus_half[:, :], ALU.pow).then_inc(norm_steps, 1)
                pool.wait_ge(norm_steps, 4 * b + 3)
                pool.tensor_tensor(shift[:, :], neg_mean[:, :], rstd[:, :], ALU.mult).then_inc(norm_steps, 1)
                wait_alone(pool, norm_steps, 4 * b + 4)

            def normalize(b, parity):
                layernorm(b)
                for t in range(TT):
                    pool.tensor_scalar(x1_hat[:, t, :], x1[parity][:, t, :], rstd[:, t:t + 1], shift[:, t:t + 1],
                                       ALU.mult, ALU.add).then_inc(x1_normed, 1)

            def kept_lo(b, c):
                for j in range(GROUP):
                    pool.wait_ge(kept_hi, (b * CT + c) * GROUP + j + 1)
                    pool.tensor_tensor(kept[c][1][:, j, :], hid[c][:, j, :], kept[c][0][:, j, :].bitcast(F32),
                                       ALU.subtract).then_inc(kept_ready, 1)

            def batch(b, parity, last=False):
                kept_lo(b, 0)
                if not last:
                    normalize(b + 1, 1 - parity)
                kept_lo(b, 1)

            normalize(0, 0)
            batch(0, 0)
            with pool.Fori(0, B // 2 - 1) as m:
                batch(2 * m + 1, 1)
                batch(2 * m + 2, 0)
            batch(B - 1, 1, last=True)

        @block.scalar
        def _(act):
            for n in range(len(loads)):
                act.wait_ge(staged[n], 16)
                act.copy(part(n, 0), stage[n][:, :]).then_inc(stage_hi, 1)

            def h_hi(b):
                for k in range(KT):
                    act.wait_ge(h2_full_ready, KT * b + k + 1)
                    act.copy(h2T[0][:, k, :], h2_full[:, k, :]).then_inc(h2_hi, 1)

            def units(b, c):
                for j in range(GROUP):
                    u = b * UNITS + c * GROUP + j
                    act.wait_ge(unit_done, u + 1)
                    act.activation(silu[j % 2][:, :], gate_ps[j % 2][:, :], ACT.Silu).then_inc(silu_done, 1)
                    act.wait_ge(hid_ready, u + 1)
                    act.activation(mag[:, j, :], hid[c][:, j, :], ACT.Abs).then_inc(mag_ready, 1)

            def kept_his(b, c):
                for j in range(GROUP):
                    act.wait_ge(kept_full, (b * CT + c) * GROUP + j + 1)
                    act.copy(kept[c][0][:, j, :], hid[c][:, j, :]).then_inc(kept_hi, 1)

            def scale_y(b, after=True):
                if after:
                    act.wait_ge(y_scaled, KT * b)
                act.copy(gate_now[:, :], mods[:, 2 * GB:2 * GB + 2, bass.ds(b, 1)].rearrange("p m o -> p (m o)"))\
                   .then_inc(gate_picked, 1)
                act.wait_ge(gate_picked, b + 1)
                act.wait_ge(down_summed, b + 1)
                for k in range(KT):
                    act.activation(y_T[:, k, :], down_ps[k][:, :], ACT.Copy, scale=gate_now[:, k:k + 1])\
                       .then_inc(y_scaled, 1)

            def batch(b, first=False, last=False, after=True):
                units(b, 0)
                kept_his(b, 0)
                if not first:
                    scale_y(b - 1, after)
                units(b, 1)
                if not last:
                    h_hi(b + 1)
                kept_his(b, 1)

            h_hi(0)
            batch(0, first=True)
            batch(1, after=False)
            with act.Fori(2, B - 1) as b:
                batch(b)
            batch(B - 1, last=True)
            scale_y(B - 1)

        @block.vector
        def _(dve):
            for n in range(len(loads)):
                dve.wait_ge(stage_hi, n + 1)
                dve.tensor_tensor(part(n, 1), stage[n][:, :], part(n, 0).bitcast(F32),
                                  ALU.subtract).then_inc(weights_ready, 1)

            def residual(b, parity, turn):
                dve.wait_ge(x_loaded, 16 * b + 16)
                for k in range(KT):
                    dve.wait_ge(turned, turn + k + 1)
                    dve.tensor_tensor(x1[parity][:, 2 * k:2 * k + 2, :],
                                      turn_ps[k][:, :].rearrange("p (t d) -> p t d", t=2),
                                      x2[:, 2 * k:2 * k + 2, :], ALU.add).then_inc(x1_ready, 1)
                dve.wait_ge(x1_ready, KT * b + KT)
                for t in range(TT):
                    dve.bn_stats(bn[:, t, :], x1[parity][:, t, :]).then_inc(stats_steps, 1)
                wait_alone(dve, stats_steps, TT * b + TT)
                for t in range(TT):
                    last = dve.bn_aggr(mv[:, t, :], bn[:, t, :])
                last.then_inc(stats_ready, 1)

            def modulate(b, turn):
                dve.tensor_copy(mod_ln[:, 0:2], mods[:, 2 * CB:2 * CB + 2, bass.ds(b, 1)].rearrange("p m o -> p (m o)"))\
                   .then_inc(mod_picked, 1)
                dve.tensor_copy(mod_ln[:, 2:4], mods[:, 2 * SB:2 * SB + 2, bass.ds(b, 1)].rearrange("p m o -> p (m o)"))\
                   .then_inc(mod_picked, 1)
                dve.wait_ge(mod_picked, 2 * b + 2)
                for k in range(KT):
                    dve.wait_ge(turned, turn + k + 1)
                    dve.tensor_scalar(h2_full[:, k, :], turn_ps[k][:, :], mod_ln[:, k:k + 1],
                                      mod_ln[:, 2 + k:3 + k], ALU.mult, ALU.add).then_inc(h2_full_ready, 1)
                for k in range(KT):
                    dve.wait_ge(h2_hi, KT * b + k + 1)
                    dve.tensor_tensor(h2T[1][:, k, :], h2_full[:, k, :], h2T[0][:, k, :].bitcast(F32),
                                      ALU.subtract).then_inc(h2_ready, 1)

            def hidden(b, c, members=range(GROUP)):
                for j in members:
                    dve.wait_ge(silu_done, b * UNITS + c * GROUP + j + 1)
                    dve.tensor_tensor(hid[c][:, j, :], up_ps[j % 2][:, :], silu[j % 2][:, :], ALU.mult)\
                       .then_inc(hid_ready, 1)

            def sparsify(b, c):
                steps = 11 * (b * CT + c)
                dve.wait_ge(mag_ready, (b * CT + c) * GROUP + GROUP)
                first = {0: 0, 1: 3, 2: 5}
                for i in range(GROUP - 1):
                    n = GROUP - 1 - i
                    dve.tensor_tensor(beats[:, first[i]:first[i] + n, :],
                                      mag[:, i:i + 1, :].to_broadcast([P, n, S]),
                                      mag[:, i + 1:GROUP, :], ALU.is_ge).then_inc(rank_steps, 1)
                dve.wait_ge(rank_steps, steps + 3)
                c01, c02, c03, c12, c13, c23 = (beats[:, n, :] for n in range(6))
                dve.tensor_tensor(wins[:, 0, :], c01, c02, ALU.add).then_inc(rank_steps, 1)
                dve.tensor_tensor(wins[:, 1, :], c12, c13, ALU.add).then_inc(rank_steps, 1)
                dve.tensor_tensor(wins[:, 2, :], c23, c02, ALU.subtract).then_inc(rank_steps, 1)
                dve.tensor_tensor(wins[:, 3, :], c13, c23, ALU.add).then_inc(rank_steps, 1)
                dve.wait_ge(rank_steps, steps + 7)
                dve.tensor_tensor(wins[:, 0, :], wins[:, 0, :], c03, ALU.add).then_inc(rank_steps, 1)
                dve.tensor_tensor(wins[:, 1, :], wins[:, 1, :], c01, ALU.subtract).then_inc(rank_steps, 1)
                dve.tensor_tensor(wins[:, 2, :], wins[:, 2, :], c12, ALU.subtract).then_inc(rank_steps, 1)
                dve.tensor_tensor(wins[:, 3, :], wins[:, 3, :], c03, ALU.add).then_inc(rank_steps, 1)
                dve.wait_ge(rank_steps, steps + 11)
                for j, (op, at) in enumerate(((ALU.is_ge, 2.0), (ALU.is_ge, 1.0), (ALU.is_ge, 0.0), (ALU.is_le, 1.0))):
                    dve.scalar_tensor_tensor(out=hid[c][:, j, :], in0=wins[:, j, :], scalar=at, in1=hid[c][:, j, :],
                                             op0=op, op1=ALU.mult).then_inc(kept_full, 1)

            def final(b, parity, turn):
                for k in range(KT):
                    dve.wait_ge(turned, turn + k + 1)
                    dve.tensor_tensor(y_out[:, 2 * k:2 * k + 2, :], turn_ps[k][:, :].rearrange("p (t d) -> p t d", t=2),
                                      x1[parity][:, 2 * k:2 * k + 2, :], ALU.add).then_inc(y_ready, 1)

            residual(0, 0, 0)
            modulate(0, 2)
            hidden(0, 0)
            sparsify(0, 0)
            hidden(0, 1, range(2))
            residual(1, 1, 4)
            hidden(0, 1, range(2, GROUP))
            modulate(1, 6)
            sparsify(0, 1)

            def later(b, parity, last=False, stores=True):
                turn = 8 + 6 * (b - 1)
                hidden(b, 0)
                sparsify(b, 0)
                hidden(b, 1, range(2))
                if stores:
                    dve.wait_ge(stored, 16 * (b - 1))
                final(b - 1, 1 - parity, turn)
                if not last:
                    residual(b + 1, 1 - parity, turn + 2)
                hidden(b, 1, range(2, GROUP))
                if not last:
                    modulate(b + 1, turn + 4)
                sparsify(b, 1)

            later(1, 1, stores=False)
            with dve.Fori(0, (B - 2) // 2 - 1) as m:
                later(2 * m + 2, 0)
                later(2 * m + 3, 1)
            later(B - 2, 0)
            later(B - 1, 1, last=True)
            dve.wait_ge(stored, 16 * (B - 1))
            final(B - 1, 1, 8 + 6 * (B - 2) + 2)

        @block.tensor
        def _(pe):
            pe.wait_ge(constants, 3)

            def turn_attn(b):
                pe.wait_ge(attn_loaded, 16 * b + 16)
                for n in range(KT):
                    for t in range(2):
                        for k in range(KT):
                            mm = pe.transpose(turn_ps[n][:, t * D + k * P:t * D + (k + 1) * P],
                                              attn_in[:, k, (2 * n + t) * P:(2 * n + t + 1) * P], ident[:, :])
                    mm.then_inc(turned, 1)

            def turn_h(b):
                pe.wait_ge(x1_normed, TT * b + TT)
                for k in range(KT):
                    for t in range(TT):
                        mm = pe.transpose(turn_ps[k][:, t * P:(t + 1) * P], x1_hat[:, t, k * P:(k + 1) * P], ident[:, :])
                    mm.then_inc(turned, 1)

            def turn_y(b):
                pe.wait_ge(y_scaled, KT * b + KT)
                for n in range(KT):
                    for t in range(2):
                        for k in range(KT):
                            mm = pe.transpose(turn_ps[n][:, t * D + k * P:t * D + (k + 1) * P],
                                              y_T[:, k, (2 * n + t) * P:(2 * n + t + 1) * P], ident[:, :])
                    mm.then_inc(turned, 1)

            def gate_up(b, c, members=range(GROUP)):
                pe.wait_ge(h2_ready, KT * b + KT)
                for j in members:
                    u = b * UNITS + c * GROUP + j
                    if not (isinstance(u, int) and u < 2):
                        pe.wait_ge(hid_ready, u - 1)
                    cols = slice((c * GROUP + j) * P, (c * GROUP + j + 1) * P)
                    for w, bank in ((wg, gate_ps[j % 2]), (wu, up_ps[j % 2])):
                        terms = []
                        for k in range(KT):
                            terms += split_passes(w[0][:, k, cols], w[1][:, k, cols], h2T[0][:, k, :], h2T[1][:, k, :])
                        for n, (l, r) in enumerate(terms):
                            mm = pe.matmul(bank[:, :], l, r, start=(n == 0), stop=(n == len(terms) - 1))
                    mm.then_inc(unit_done, 1)

            def down(b, c, free=True):
                if c == 0 and free:
                    pe.wait_ge(y_scaled, KT * b)
                for j in range(GROUP):
                    pe.wait_ge(kept_ready, (b * CT + c) * GROUP + j + 1)
                    for k in range(KT):
                        cols = slice(k * P, (k + 1) * P)
                        t = c * GROUP + j
                        for n, (l, r) in enumerate(split_passes(wd[0][:, t, cols], wd[1][:, t, cols],
                                                                kept[c][0][:, j, :], kept[c][1][:, j, :])):
                            mm = pe.matmul(down_ps[k][:, :], l, r, start=(c == 0 and j == 0 and n == 0),
                                           stop=(c == CT - 1 and j == GROUP - 1 and n == 2))
                if c == CT - 1:
                    mm.then_inc(down_summed, 1)

            turn_attn(0)
            pe.wait_ge(x1_ready, KT)
            turn_h(0)
            pe.wait_ge(weights_ready, len(loads))
            gate_up(0, 0)
            gate_up(0, 1, range(2))
            turn_attn(1)
            gate_up(0, 1, range(2, GROUP))
            pe.wait_ge(x1_ready, 2 * KT)
            turn_h(1)
            down(0, 0, free=False)

            def later(b, last=False):
                gate_up(b, 0)
                down(b - 1, 1)
                gate_up(b, 1, range(2))
                turn_y(b - 1)
                if not last:
                    pe.wait_ge(y_ready, KT * b)
                    turn_attn(b + 1)
                gate_up(b, 1, range(2, GROUP))
                if not last:
                    pe.wait_ge(x1_ready, KT * b + 2 * KT)
                    turn_h(b + 1)
                down(b, 0)

            with pe.Fori(1, B - 1) as b:
                later(b)
            later(B - 1, last=True)
            down(B - 1, 1)
            pe.wait_ge(y_ready, KT * (B - 1))
            turn_y(B - 1)


def build(nc, x, wqT, wkT, wvT, woT, wg, wu, wd, cT, wmod, out):
    attn_T = nc.dram_tensor("attn_T", (B, D, S), F32, kind="Internal").ap()
    with nc.sbuf_tensor("mods", [P, 12, B + 1], F32) as mods:
        attention_phase(nc, x, cT, wmod, wqT, wkT, wvT, woT, attn_T, mods)
        mlp_phase(nc, x, attn_T, wg, wu, wd, out, mods)


def kernel(**inputs):
    import concourse.bacc as bacc
    from concourse.bass_utils import run_bass_kernel_spmd as run

    def by_partition(w):
        t = w.shape[0] // P
        return w.reshape(t, P, w.shape[1]).transpose(1, 0, 2).reshape(P, t * w.shape[1])

    def grouped(w):
        return w.reshape(w.shape[0], CT, P, GROUP).transpose(0, 1, 3, 2).reshape(w.shape[0], I)

    a = {k: np.asarray(val) for k, val in inputs.items()}
    wd = a["L0_ffn_w_down"].reshape(CT, P, GROUP, D).transpose(1, 0, 2, 3).reshape(P, CT * GROUP * D)
    arrays = {
        "x": a["L0_attn_resid_pre"],
        "wqT": by_partition(a["L0_attn_Wq"].T),
        "wkT": by_partition(a["L0_attn_Wk"].T),
        "wvT": by_partition(a["L0_attn_Wv"].T),
        "woT": by_partition(a["L0_attn_Wo"].T),
        "wg": by_partition(grouped(a["L0_ffn_w_gate"])),
        "wu": by_partition(grouped(a["L0_ffn_w_up"])),
        "wd": wd,
        "cT": a["L0_c"].T.reshape(KT, P, B).transpose(1, 0, 2),
        "wmod": a["L0_wmod"].reshape(KT, P, 6 * D).transpose(1, 0, 2),
    }
    arrays = {k: np.ascontiguousarray(val) for k, val in arrays.items()}
    nc = bacc.Bacc("TRN2", target_bir_lowering=False, num_devices=1)
    args = [nc.dram_tensor(k, val.shape, F32, kind="ExternalInput").ap() for k, val in arrays.items()]
    out = nc.dram_tensor("out", (B, S, D), F32, kind="ExternalOutput").ap()
    build(nc, *args, out)
    r = run(nc, [arrays], core_ids=[0])
    return r.results[0]["out"]
```

```python
import math
from contextlib import ExitStack

import numpy as np

import concourse.bass as bass
from concourse import mybir

F32 = mybir.dt.float32
F32R = mybir.dt.float32r
BF16 = mybir.dt.bfloat16
ACT = mybir.ActivationFunctionType
ALU = mybir.AluOpType

P = 128
B, S, D = 8, 512, 256
H, DH = 16, 128
HD = H * DH
I = 1024
KT = D // P
TT = S // P
GROUP = 4
CT = I // P // GROUP
LN_EPS = 1e-5
CLIP = 1024.0
MASKED = -1e30
SA, CA, GA, SB, CB, GB = range(6)

SLOPE = [float(np.float32((2 ** (-2 ** (-(math.log2(H) - 3)))) ** (h + 1))) for h in range(H)]

AREA = {3: 0, 2: 512, 0: 896, 1: 1024}
BANKS = [[3], [2, 0], [1]]
BANK_COLS = [(0, 512), (512, 1024), (1024, 1280)]
BLOCK_ORDER = [3, 2, 0, 1]
WIDTH = {i: P * (i + 1) for i in range(TT)}
KEY_AREA = {j: AREA[TT - 1 - j] for j in range(TT)}
KEY_BANKS = [[TT - 1 - i for i in blocks] for blocks in BANKS]
TRI = 1280


def wait_alone(eng, semaphore, value):
    eng.wait_ge(semaphore, value)
    eng.nop(nofuse=True)


def split_passes(hi_l, lo_l, hi_r, lo_r):
    return [(hi_l, hi_r), (hi_l, lo_r), (lo_l, hi_r)]


RING = 6


def next_head(h):
    return (h + 1) % H


def previous_head(h):
    return (h - 1) % H


def v_halves(h, last=False):
    if h == H - 1 and last:
        return []
    if h == H - 1:
        return [(("v", H - 2), 0, 0), (("v", H - 1), 0, 2)]
    return [] if h == H - 2 else [(("v", h), h // 2 + 1, 2 * (h % 2))]


def slot_uses(h, first=False, last=False):
    uses = [("s", h, n) for n in range(3)]
    if not first:
        uses.append(("z", previous_head(h)))
    if not (last and h == H - 1):
        uses += [("q", next_head(h)), ("k", next_head(h))]
    if h == H - 2 and not last:
        uses += [("ln", 0), ("ln", 1)]
    return uses + [use for use, _, _ in v_halves(h, last)] + [("t", h, n) for n in range(3)]


PRE_USES = [("ln", 0), ("ln", 1), ("q", 0), ("k", 0), ("v", H - 2), ("v", H - 1)] + slot_uses(0, first=True)
USES = sum([slot_uses(h) for h in list(range(1, H)) + [0]], [])
LAST_USES = sum([slot_uses(h, last=True) for h in range(1, H)], []) + [("z", H - 1)]
PER_BATCH = len(USES)
assert PER_BATCH % RING == 0
PRE_USE = {u: n for n, u in enumerate(PRE_USES)}
USE = {u: n for n, u in enumerate(USES)}
LAST_USE = {u: n for n, u in enumerate(LAST_USES)}
LAST = B - 1
PRE = None


def has_hi(use):
    return use[0] not in ("ln", "s")


def ring_use(b, key):
    if b is PRE:
        return PRE_USE[key], PRE_USE[key]
    use = (LAST_USE if isinstance(b, int) else USE)[key]
    return len(PRE_USES) + use, len(PRE_USES) + b * PER_BATCH + use


def use_before(b, key):
    return len(PRE_USES) + b * PER_BATCH + USE[key] - PER_BATCH


def hi_count(b, key):
    in_pre = [u for u in PRE_USES if has_hi(u)]
    in_loop = [u for u in USES if has_hi(u)]
    if b is PRE:
        return in_pre.index(key) + 1
    here = [u for u in LAST_USES if has_hi(u)] if isinstance(b, int) else in_loop
    return len(in_pre) + b * len(in_loop) + here.index(key) + 1


def heads_before(b, h):
    if b is PRE:
        return 0
    return b * H + (h if h else H)


def attention_phase(nc, x, cT, wmod, wqT, wkT, wvT, woT, attn_T, mods):
    with ExitStack() as ctx:
        def sb(name, shape, dt):
            return ctx.enter_context(nc.sbuf_tensor(name, shape, dt))

        def sem(name):
            return ctx.enter_context(nc.semaphore(name))

        wq = [sb(f"wq_{s}", [P, KT, HD], F32R) for s in ("hi", "lo")]
        wk = [sb(f"wk_{s}", [P, KT, HD], F32R) for s in ("hi", "lo")]
        wv = [sb(f"wv_{s}", [P, KT, HD], F32R) for s in ("hi", "lo")]
        wo = [sb(f"wo_{s}", [P, H, D], F32R) for s in ("hi", "lo")]
        hT = [sb(f"hT_{s}", [P, KT, S], F32R) for s in ("hi", "lo")]
        qT = [sb(f"qT_{s}", [P, S], F32R) for s in ("hi", "lo")]
        kT = [sb(f"kT_{s}", [P, S], F32R) for s in ("hi", "lo")]
        zT = [sb(f"zT_{s}", [P, S], F32R) for s in ("hi", "lo")]
        v = [sb(f"v_{s}", [P, 2, TT, 2 * DH], F32R) for s in ("hi", "lo")]
        pT = [sb(f"pT_{s}", [P, TRI], F32R) for s in ("hi", "lo")]
        probs = sb("probs", [P, TRI], F32)
        key_pos = sb("key_pos", [P, TRI], F32)
        xin = sb("xin", [P, TT, D], F32)
        h_full = sb("h_full", [P, KT, S], F32)
        out_T = sb("out_T", [P, KT, S], F32)
        ident = sb("ident", [P, P], F32)
        stage = [sb(f"stage{i}", [P, 1024], F32)[:, :] for i in range(2)]
        stage += [probs[:, 0:1024], out_T[:, :, :].rearrange("p k n -> p (k n)")]
        MOD_CHUNKS = 3
        mod_stage = [h_full, out_T, h_full]
        c_sb = sb("c_sb", [P, KT, B], F32)
        c_exp = sb("c_exp", [P, KT, B], F32)
        c_silu = sb("c_silu", [P, KT, B], F32)
        mod_sign = sb("mod_sign", [P, 2, B], F32)
        mod_abs = sb("mod_abs", [P, 2, B], F32)
        mod_ln = sb("mod_ln", [P, 4], F32)
        gate_now = sb("gate_now", [P, KT], F32)
        neg_max = sb("neg_max", [P, TT], F32)
        row_sum = sb("row_sum", [P, TT], F32)
        row_inv = sb("row_inv", [P, TT], F32)
        bn = sb("bn", [P, TT, 6], F32)
        mv = sb("mv", [P, TT, 2], F32)
        var_eps = sb("var_eps", [P, TT], F32)
        minus_half = sb("minus_half", [P, TT], F32)
        rstd = sb("rstd", [P, TT], F32)
        neg_mean = sb("neg_mean", [P, TT], F32)
        shift = sb("shift", [P, TT], F32)

        out_ps = [ctx.enter_context(nc.psum_tensor(f"out_ps{i}", [P, S], F32)) for i in range(KT)]
        ring = [ctx.enter_context(nc.psum_tensor(f"ring{i}", [P, 512], F32)) for i in range(RING)]

        staged = [sem(f"staged{i}") for i in range(len(stage))]
        mod_staged = [sem(f"mod_staged{i}") for i in range(MOD_CHUNKS)]
        mods_summed = sem("mods_summed")
        c_loaded = sem("c_loaded")
        stage_hi = sem("stage_hi")
        stage_free = sem("stage_free")
        c_exp_done = sem("c_exp_done")
        c_steps = sem("c_steps")
        c_ready = sem("c_ready")
        mods_steps = sem("mods_steps")
        constants = sem("constants")
        x_loaded = sem("x_loaded")
        stats_steps = sem("stats_steps")
        stats_ready = sem("stats_ready")
        norm_steps = sem("norm_steps")
        x_normed = sem("x_normed")
        mod_picked = sem("mod_picked")
        hT_hi = sem("hT_hi")
        hT_ready = sem("hT_ready")
        ring_filled = sem("ring_filled")
        ring_hi = sem("ring_hi")
        ring_freed = sem("ring_freed")
        max_ready = sem("max_ready")
        exp_done = sem("exp_done")
        inv_ready = sem("inv_ready")
        probs_ready = sem("probs_ready")
        out_summed = sem("out_summed")
        gate_picked = sem("gate_picked")
        out_taken = sem("out_taken")
        out_T_free = sem("out_T_free")

        weights = [(wqT, wq), (wkT, wk), (wvT, wv), (woT, wo)]
        W_ORDER = [(w, c) for w in range(3) for c in (0, 2)] + [(w, c) for w in range(3) for c in (1, 3)] \
            + [(3, c) for c in range(4)]
        FIRST = 6
        CHUNKS = len(W_ORDER)
        BUFFER = [n % 3 for n in range(FIRST)] + [(n + 3) % 4 for n in range(CHUNKS - FIRST)]
        USED_BEFORE = [max([m for m in range(n) if BUFFER[m] == BUFFER[n]], default=None) for n in range(CHUNKS)]
        ROUND = [BUFFER[:n + 1].count(BUFFER[n]) for n in range(CHUNKS)]

        def weight_chunk(n, s):
            w, c = W_ORDER[n]
            return weights[w][1][s][:, :, :].rearrange("p a n -> p (a n)")[:, c * 1024:(c + 1) * 1024]

        def ring_as(use, like):
            bank = ring[use % RING]
            return bank[:, :].rearrange("p (t n) -> p t n", t=2) if len(like.shape) == 3 else bank[:, 0:like.shape[1]]

        def slope_scale(h):
            return 1.0 / (math.sqrt(DH) * SLOPE[h])

        block = ctx.enter_context(nc.Block())

        @block.sync
        def _(sp):
            sp.dma_start(c_sb[:, :, :], cT).then_inc(c_loaded, 16)
            sp.dma_start(xin[:, :, :], x[0].rearrange("(t p) d -> p t d", p=P)).then_inc(x_loaded, 16)
            for n, (w, c) in enumerate(W_ORDER):
                if USED_BEFORE[n] is not None:
                    sp.wait_ge(stage_free, USED_BEFORE[n] + 1)
                elif n >= FIRST:
                    sp.wait_ge(mods_summed, MOD_CHUNKS)
                sp.dma_start(stage[BUFFER[n]], weights[w][0][:, c * 1024:(c + 1) * 1024]).then_inc(staged[BUFFER[n]], 16)
                if n < MOD_CHUNKS:
                    if n == 2:
                        sp.wait_ge(mods_summed, 1)
                    sp.dma_start(mod_stage[n][:, :, :], wmod[:, :, n * 512:(n + 1) * 512]).then_inc(mod_staged[n], 16)

            def step(b, load):
                if load:
                    sp.wait_ge(hT_ready, 2 * b + 2)
                    sp.dma_start(xin[:, :, :],
                                 x[bass.ds(b + 1, 1)].rearrange("o (t p) d -> p (o t) d", p=P)).then_inc(x_loaded, 16)
                sp.wait_ge(out_taken, KT * (b + 2))
                sp.dma_start(attn_T[bass.ds(b, 1)].rearrange("o (k p) n -> p (o k) n", p=P),
                             out_T[:, :, :]).then_inc(out_T_free, 16)

            with sp.Fori(0, B - 1) as b:
                step(b, True)
            sp.wait_ge(out_taken, KT * (B + 1))
            sp.dma_start(attn_T[B - 1].rearrange("(k p) n -> p k n", p=P), out_T[:, :, :]).then_inc(out_T_free, 16)
            sp.wait_ge(out_T_free, 16 * (B + 1))

        @block.gpsimd
        def _(pool):
            pool.memset(row_sum[:, :], 0.0).then_inc(out_T_free, 16)
            pool.memset(minus_half[:, :], -0.5).then_inc(constants, 1)
            pool.memset(mods[:, :, :], 0.0).then_inc(constants, 1)
            pool.memset(ident[:, :], 0.0).then_inc(constants, 1)
            pool.iota(key_pos[:, 0:512], pattern=[[1, 512]], base=0, channel_multiplier=0,
                      allow_small_or_imprecise_dtypes=True).then_inc(constants, 1)
            pool.wait_ge(constants, 4)
            pool.affine_select(out=ident[:, :], in_=ident[:, :], compare_op=ALU.not_equal, fill=1.0, base=0,
                               pattern=[[-1, P]], channel_multiplier=1).then_inc(constants, 1)
            for i in range(TT - 1):
                pool.tensor_copy(key_pos[:, AREA[i]:AREA[i] + WIDTH[i]], key_pos[:, 0:WIDTH[i]]).then_inc(constants, 1)
            pool.wait_ge(constants, 8)
            for i in range(TT):
                diag = key_pos[:, AREA[i] + P * i:AREA[i] + P * (i + 1)]
                pool.affine_select(out=diag, in_=diag, compare_op=ALU.is_ge, fill=MASKED, base=0,
                                   pattern=[[-1, P]], channel_multiplier=1).then_inc(constants, 1)

            def layernorm(count):
                wait_alone(pool, stats_ready, count)
                pool.tensor_scalar(var_eps[:, :], mv[:, :, 1], LN_EPS, 1.0, ALU.add, ALU.mult).then_inc(norm_steps, 1)
                pool.tensor_scalar(neg_mean[:, :], mv[:, :, 0], -1.0, 1.0, ALU.mult, ALU.mult).then_inc(norm_steps, 1)
                pool.wait_ge(norm_steps, 4 * count - 2)
                pool.tensor_tensor(rstd[:, :], var_eps[:, :], minus_half[:, :], ALU.pow).then_inc(norm_steps, 1)
                pool.wait_ge(norm_steps, 4 * count - 1)
                pool.tensor_tensor(shift[:, :], neg_mean[:, :], rstd[:, :], ALU.mult).then_inc(norm_steps, 1)
                wait_alone(pool, norm_steps, 4 * count)
                for t in range(TT):
                    pool.tensor_scalar(xin[:, t, :], xin[:, t, :], rstd[:, t:t + 1], shift[:, t:t + 1],
                                       ALU.mult, ALU.add).then_inc(x_normed, 1)

            def slot(b, h):
                heads = heads_before(b, h)
                for n, i in enumerate(BLOCK_ORDER):
                    if n in (0, 3):
                        wait_alone(pool, inv_ready, heads * 2 + (1 if n == 0 else 2))
                    blk = probs[:, AREA[i]:AREA[i] + WIDTH[i]]
                    pool.tensor_scalar(blk, blk, row_inv[:, n:n + 1], 1.0, ALU.mult, ALU.mult).then_inc(probs_ready, 1)
                if h == 7 and b is not LAST:
                    layernorm(b + 2)
                if h == H - 2 and b is not LAST:
                    h_lo(b + 2)

            def h_lo(count):
                for k in range(KT):
                    pool.wait_ge(hT_hi, KT * (count - 1) + k + 1)
                    pool.tensor_tensor(hT[1][:, k, :], h_full[:, k, :], hT[0][:, k, :].bitcast(F32),
                                       ALU.subtract).then_inc(hT_ready, 1)

            layernorm(1)
            h_lo(1)
            slot(PRE, 0)
            with pool.Fori(0, LAST) as b:
                for h in range(1, H):
                    slot(b, h)
                slot(b, 0)
            for h in range(1, H):
                slot(LAST, h)

        @block.scalar
        def _(act):
            act.wait_ge(c_loaded, 16)
            act.activation(c_exp[:, :, :], c_sb[:, :, :], ACT.Exp, scale=-1.0).then_inc(c_exp_done, 1)

            def weight_hi(ns):
                for n in ns:
                    act.wait_ge(staged[BUFFER[n]], 16 * ROUND[n])
                    act.copy(weight_chunk(n, 0), stage[BUFFER[n]]).then_inc(stage_hi, 1)

            def hi(b, key, dst, scale=1.0):
                static, count = ring_use(b, key)
                act.wait_ge(ring_filled, count + 1)
                act.activation(dst, ring_as(static, dst), ACT.Copy, scale=scale).then_inc(ring_hi, 1)

            def h_hi(b, count):
                for k in range(KT):
                    act.wait_ge(ring_freed, ring_use(b, ("ln", k))[1] + 1)
                    act.copy(hT[0][:, k, :], h_full[:, k, :]).then_inc(hT_hi, 1)

            def slot(b, h):
                heads = heads_before(b, h)
                for n, i in enumerate(BLOCK_ORDER):
                    blk = probs[:, AREA[i]:AREA[i] + WIDTH[i]]
                    act.wait_ge(max_ready, heads * TT + n + 1)
                    act.activation(blk, blk, ACT.Exp, bias=neg_max[:, i:i + 1], scale=-1.0,
                                   accum_out=row_sum[:, n:n + 1]).then_inc(exp_done, 1)
                    if b is not PRE and n == 2:
                        hi(b, ("z", previous_head(h)), zT[0][:, :])
                last = b is LAST
                if not (last and h == H - 1):
                    hi(b, ("q", next_head(h)), qT[0][:, :], slope_scale(next_head(h)))
                    hi(b, ("k", next_head(h)), kT[0][:, :])
                if h == H - 2 and not last:
                    h_hi(b, b + 2)
                for key, pair, half in v_halves(h, last):
                    hi(b, key, v[0][:, pair % 2, half:half + 2, :])
                for n, (start, end) in enumerate(BANK_COLS):
                    hi(b, ("t", h, n), pT[0][:, start:end])

            weight_hi(range(0, 4))
            h_hi(PRE, 1)
            weight_hi(range(4, 10))
            hi(PRE, ("q", 0), qT[0][:, :], slope_scale(0))
            hi(PRE, ("k", 0), kT[0][:, :])
            hi(PRE, ("v", H - 2), v[0][:, 0, 0:2, :])
            hi(PRE, ("v", H - 1), v[0][:, 0, 2:4, :])
            weight_hi(range(10, CHUNKS))
            act.wait_ge(stage_free, CHUNKS)
            slot(PRE, 0)

            def pick_gates(b):
                act.wait_ge(out_taken, KT * (b + 1))
                act.copy(gate_now[:, :], mods[:, 2 * GA:2 * GA + 2, bass.ds(b, 1)]
                         .rearrange("p m o -> p (m o)")).then_inc(gate_picked, 1)

            def take_out(b):
                act.wait_ge(out_summed, b + 1)
                act.wait_ge(out_T_free, 16 * b + 16)
                act.wait_ge(gate_picked, b + 1)
                act.activation(out_T[:, 0, :], out_ps[0][:, :], ACT.Copy, scale=gate_now[:, 0:1]).then_inc(out_taken, 1)
                act.activation(out_T[:, 1, :], out_ps[1][:, :], ACT.Copy, scale=gate_now[:, 1:2]).then_inc(out_taken, 1)

            with act.Fori(0, LAST) as b:
                pick_gates(b)
                for h in range(1, H):
                    slot(b, h)
                slot(b, 0)
                take_out(b)
            pick_gates(LAST)
            for h in range(1, H):
                slot(LAST, h)
            hi(LAST, ("z", H - 1), zT[0][:, :])
            take_out(LAST)

        @block.vector
        def _(dve):
            dve.wait_ge(c_exp_done, 1)
            dve.tensor_scalar(c_exp[:, :, :], c_exp[:, :, :], 1.0, None, ALU.add).then_inc(c_steps, 1)
            dve.wait_ge(c_steps, 1)
            dve.reciprocal(c_exp[:, :, :], c_exp[:, :, :]).then_inc(c_steps, 1)
            dve.wait_ge(c_steps, 2)
            dve.tensor_tensor(c_silu[:, :, :], c_sb[:, :, :], c_exp[:, :, :], ALU.mult).then_inc(c_ready, 1)

            def weight_lo(ns):
                for n in ns:
                    dve.wait_ge(stage_hi, n + 1)
                    dve.tensor_tensor(weight_chunk(n, 1), stage[BUFFER[n]], weight_chunk(n, 0).bitcast(F32),
                                      ALU.subtract).then_inc(stage_free, 1)

            def statistics(count, tiles=range(TT)):
                if tiles[0] == 0:
                    dve.wait_ge(x_loaded, 16 * count)
                for t in tiles:
                    dve.bn_stats(bn[:, t, :], xin[:, t, :]).then_inc(stats_steps, 1)
                if tiles[-1] == TT - 1:
                    wait_alone(dve, stats_steps, TT * count)
                    for t in range(TT):
                        last = dve.bn_aggr(mv[:, t, :], bn[:, t, :])
                    last.then_inc(stats_ready, 1)

            statistics(1)
            weight_lo(range(0, 4))
            dve.wait_ge(mods_summed, MOD_CHUNKS)
            dve.wait_ge(constants, 4)
            dve.tensor_copy(mods[:, :, 0:B], out_ps[0][:, 0:12 * B].rearrange("p (m b) -> p m b", b=B)).then_inc(out_taken, KT)
            dve.wait_ge(out_taken, KT)
            for k in (CA, CB):
                m = mods[:, 2 * k:2 * k + 2, 0:B]
                dve.tensor_scalar(m, m, 1.0, None, ALU.add).then_inc(mods_steps, 1)
            for n, k in enumerate((GA, GB)):
                m = mods[:, 2 * k:2 * k + 2, 0:B]
                dve.tensor_scalar(mod_sign[:, :, :], m, 0.0, 2.0, ALU.is_ge, ALU.mult).then_inc(mods_steps, 1)
                dve.scalar_tensor_tensor(out=mod_abs[:, :, :], in0=m, scalar=-1.0, in1=m, op0=ALU.mult,
                                         op1=ALU.max).then_inc(mods_steps, 1)
                dve.wait_ge(mods_steps, 4 + 4 * n)
                dve.tensor_scalar(mod_abs[:, :, :], mod_abs[:, :, :], 0.25, None, ALU.max).then_inc(mods_steps, 1)
                dve.wait_ge(mods_steps, 5 + 4 * n)
                dve.scalar_tensor_tensor(out=m, in0=mod_sign[:, :, :], scalar=-1.0, in1=mod_abs[:, :, :],
                                         op0=ALU.add, op1=ALU.mult).then_inc(mods_steps, 1)
                dve.wait_ge(mods_steps, 6 + 4 * n)

            def modulate(b, batch, count):
                dve.tensor_copy(mod_ln[:, 0:2], mods[:, 2 * CA:2 * CA + 2, batch].rearrange("p m o -> p (m o)"))\
                   .then_inc(mod_picked, 1)
                dve.tensor_copy(mod_ln[:, 2:4], mods[:, 2 * SA:2 * SA + 2, batch].rearrange("p m o -> p (m o)"))\
                   .then_inc(mod_picked, 1)
                dve.wait_ge(mod_picked, 2 * count)
                for k in range(KT):
                    static, number = ring_use(b, ("ln", k))
                    dve.wait_ge(ring_filled, number + 1)
                    dve.tensor_scalar(h_full[:, k, :], ring[static % RING][:, :], mod_ln[:, k:k + 1],
                                      mod_ln[:, 2 + k:3 + k], ALU.mult, ALU.add).then_inc(ring_freed, 1)

            def lo(b, key, parts, scale=None):
                static = ring_use(b, key)[0]
                dve.wait_ge(ring_hi, hi_count(b, key))
                if scale is None:
                    dve.tensor_tensor(parts[1], ring_as(static, parts[1]), parts[0].bitcast(F32),
                                      ALU.subtract).then_inc(ring_freed, 1)
                else:
                    dve.scalar_tensor_tensor(out=parts[1], in0=ring_as(static, parts[1]), scalar=scale,
                                             in1=parts[0].bitcast(F32), op0=ALU.mult,
                                             op1=ALU.subtract).then_inc(ring_freed, 1)

            def slot(b, h):
                heads = heads_before(b, h)
                limit = CLIP / SLOPE[h]
                for n, (start, end) in enumerate(BANK_COLS):
                    static, number = ring_use(b, ("s", h, n))
                    dve.wait_ge(ring_filled, number + 1)
                    dve.tensor_scalar(probs[:, start:end], ring[static % RING][:, 0:end - start],
                                      limit, -limit, ALU.min, ALU.max).then_inc(ring_freed, 1)
                    wait_alone(dve, ring_freed, number + 1)
                    for i in BANKS[n]:
                        blk = probs[:, AREA[i]:AREA[i] + WIDTH[i]]
                        dve.tensor_tensor_reduce(blk, blk, key_pos[:, AREA[i]:AREA[i] + WIDTH[i]], -SLOPE[h], 3e38,
                                                 ALU.add, ALU.min, neg_max[:, i:i + 1]).then_inc(max_ready, 1)
                dve.wait_ge(exp_done, heads * TT + 3)
                dve.reciprocal(row_inv[:, 0:3], row_sum[:, 0:3]).then_inc(inv_ready, 1)
                if b is not PRE:
                    lo(b, ("z", previous_head(h)), [t[:, :] for t in zT])
                dve.wait_ge(exp_done, heads * TT + TT)
                dve.reciprocal(row_inv[:, 3:4], row_sum[:, 3:4]).then_inc(inv_ready, 1)
                last = b is LAST
                if not (last and h == H - 1):
                    lo(b, ("q", next_head(h)), [t[:, :] for t in qT], slope_scale(next_head(h)))
                    lo(b, ("k", next_head(h)), [t[:, :] for t in kT])
                if h == H - 2 and not last:
                    modulate(b, bass.ds(b + 1, 1), b + 2)
                for key, pair, half in v_halves(h, last):
                    lo(b, key, [t[:, pair % 2, half:half + 2, :] for t in v])
                for n, (start, end) in enumerate(BANK_COLS):
                    lo(b, ("t", h, n), [t[:, start:end] for t in pT])
                if 3 <= h < 3 + TT and not last:
                    statistics(b + 2, [h - 3])

            modulate(PRE, slice(0, 1), 1)
            weight_lo(range(4, 10))
            lo(PRE, ("q", 0), [t[:, :] for t in qT], slope_scale(0))
            lo(PRE, ("k", 0), [t[:, :] for t in kT])
            lo(PRE, ("v", H - 2), [t[:, 0, 0:2, :] for t in v])
            lo(PRE, ("v", H - 1), [t[:, 0, 2:4, :] for t in v])
            weight_lo(range(10, CHUNKS))
            dve.wait_ge(constants, 12)
            slot(PRE, 0)
            with dve.Fori(0, LAST) as b:
                for h in range(1, H):
                    slot(b, h)
                slot(b, 0)
            for h in range(1, H):
                slot(LAST, h)
            lo(LAST, ("z", H - 1), [t[:, :] for t in zT])

        @block.tensor
        def _(pe):
            pe.wait_ge(constants, 5)
            for n in range(MOD_CHUNKS):
                pe.wait_ge(mod_staged[n], 16)
                if n == 0:
                    pe.wait_ge(c_ready, 1)
                w = mod_stage[n]
                for t in range(4):
                    m = 4 * n + t
                    for k in range(KT):
                        mm = pe.matmul(out_ps[0][:, m * B:(m + 1) * B], w[:, k, t * P:(t + 1) * P], c_silu[:, k, :],
                                       start=(k == 0), stop=(k == KT - 1))
                mm.then_inc(mods_summed, 1)

            def accumulate(out, terms):
                for n, (l, r) in enumerate(terms):
                    mm = pe.matmul(out, l, r, start=(n == 0), stop=(n == len(terms) - 1))
                return mm

            def claim(b, key):
                static, number = ring_use(b, key)
                if not (b is PRE and number < RING):
                    pe.wait_ge(ring_freed, number - RING + 1)
                return ring[static % RING]

            def turn_x(b, ln_count):
                for k in range(KT):
                    bank = claim(b, ("ln", k))
                    for t in range(TT):
                        if k == 0:
                            pe.wait_ge(x_normed, TT * (ln_count - 1) + t + 1)
                        mm = pe.transpose(bank[:, t * P:(t + 1) * P], xin[:, t, k * P:(k + 1) * P], ident[:, :])
                    mm.then_inc(ring_filled, 1)

            def project(b, kind, w, h):
                bank = claim(b, (kind, h))
                cols = slice(h * DH, (h + 1) * DH)
                terms = []
                for k in range(KT):
                    terms += split_passes(w[0][:, k, cols], w[1][:, k, cols], hT[0][:, k, :], hT[1][:, k, :])
                accumulate(bank[:, :], terms).then_inc(ring_filled, 1)

            def project_v(b, key, pair, half):
                bank = claim(b, key)
                cols = slice(pair * 2 * DH, (pair + 1) * 2 * DH)
                for t in range(2):
                    rows = slice((half + t) * P, (half + t + 1) * P)
                    terms = []
                    for k in range(KT):
                        terms += split_passes(hT[0][:, k, rows], hT[1][:, k, rows], wv[0][:, k, cols], wv[1][:, k, cols])
                    mm = accumulate(bank[:, t * 256:(t + 1) * 256], terms)
                mm.then_inc(ring_filled, 1)

            def scores(b, h):
                number = use_before(b, ("k", h)) if h == 1 else ring_use(b, ("k", h))[1]
                pe.wait_ge(ring_freed, number + 1)
                for n, blocks in enumerate(BANKS):
                    bank = claim(b, ("s", h, n))
                    for i in blocks:
                        rows = slice(i * P, (i + 1) * P)
                        cols = slice(AREA[i] - BANK_COLS[n][0], AREA[i] - BANK_COLS[n][0] + WIDTH[i])
                        mm = accumulate(bank[:, cols], split_passes(qT[0][:, rows], qT[1][:, rows],
                                                                    kT[0][:, 0:WIDTH[i]], kT[1][:, 0:WIDTH[i]]))
                    mm.then_inc(ring_filled, 1)

            def turn_probs(b, h):
                pe.wait_ge(probs_ready, heads_before(b, h) * TT + TT)
                for n, keys in enumerate(KEY_BANKS):
                    bank = claim(b, ("t", h, n))
                    for j in keys:
                        for i in range(j, TT):
                            col = KEY_AREA[j] - BANK_COLS[n][0] + (i - j) * P
                            mm = pe.transpose(bank[:, col:col + P], probs[:, AREA[i] + j * P:AREA[i] + (j + 1) * P],
                                              ident[:, :])
                    mm.then_inc(ring_filled, 1)

            def attend(b, h):
                bank = claim(b, ("z", h))
                for m, keys in enumerate(KEY_BANKS):
                    number = use_before(b, ("t", h, m)) if h == 0 else ring_use(b, ("t", h, m))[1]
                    pe.wait_ge(ring_freed, number + 1)
                    for j in keys:
                        cols = slice(KEY_AREA[j], KEY_AREA[j] + S - j * P)
                        vj = [t[:, (h // 2) % 2, j, (h % 2) * DH:(h % 2 + 1) * DH] for t in v]
                        for n, (l, r) in enumerate(split_passes(vj[0], vj[1], pT[0][:, cols], pT[1][:, cols])):
                            mm = pe.matmul(bank[:, j * P:S], l, r, start=(j == 0 and n == 0),
                                           stop=(j == KEY_BANKS[-1][-1] and n == 2))
                mm.then_inc(ring_filled, 1)

            def project_out(b, h):
                pe.wait_ge(ring_freed, ring_use(b, ("z", h))[1] + 1)
                if h == 0:
                    pe.wait_ge(out_taken, KT * (b + 1))
                for k in range(KT):
                    cols = slice(k * P, (k + 1) * P)
                    terms = split_passes(wo[0][:, h, cols], wo[1][:, h, cols], zT[0][:, :], zT[1][:, :])
                    for n, (l, r) in enumerate(terms):
                        mm = pe.matmul(out_ps[k][:, :], l, r, start=(h == 0 and n == 0),
                                       stop=(h == H - 1 and n == 2))
                if h == H - 1:
                    mm.then_inc(out_summed, 1)

            def slot(b, h):
                scores(b, h)
                if b is not PRE:
                    attend(b, previous_head(h))
                last = b is LAST
                if h == H - 1 and not last:
                    pe.wait_ge(hT_ready, KT * (b + 2))
                if not (last and h == H - 1):
                    project(b, "q", wq, next_head(h))
                    project(b, "k", wk, next_head(h))
                if h == H - 2 and not last:
                    turn_x(b, b + 2)
                for key, pair, half in v_halves(h, last):
                    project_v(b, key, pair, half)
                if b is not PRE:
                    project_out(b, previous_head(h))
                turn_probs(b, h)

            turn_x(PRE, 1)
            pe.wait_ge(stage_free, FIRST)
            pe.wait_ge(hT_ready, KT)
            project(PRE, "q", wq, 0)
            project(PRE, "k", wk, 0)
            project_v(PRE, ("v", H - 2), 0, 0)
            project_v(PRE, ("v", H - 1), 0, 2)
            pe.wait_ge(stage_free, CHUNKS)
            slot(PRE, 0)
            with pe.Fori(0, LAST) as b:
                for h in range(1, H):
                    slot(b, h)
                slot(b, 0)
            for h in range(1, H):
                slot(LAST, h)
            attend(LAST, H - 1)
            project_out(LAST, H - 1)


def mlp_phase(nc, x, attn_T, wg_in, wu_in, wd_in, out, mods):
    UNITS = CT * GROUP
    with ExitStack() as ctx:
        def sb(name, shape, dt):
            return ctx.enter_context(nc.sbuf_tensor(name, shape, dt))

        def sem(name):
            return ctx.enter_context(nc.semaphore(name))

        def ps(name):
            return ctx.enter_context(nc.psum_tensor(name, [P, 512], F32))

        wg = [sb(f"wg_{s}", [P, KT, I], F32R) for s in ("hi", "lo")]
        wu = [sb(f"wu_{s}", [P, KT, I], F32R) for s in ("hi", "lo")]
        wd = [sb(f"wd_{s}", [P, UNITS, D], F32R) for s in ("hi", "lo")]
        x2 = sb("x2", [P, TT, D], F32)
        attn_in = sb("attn_in", [P, KT, S], F32)
        x1 = sb("x1", [P, B, TT, D], F32)
        x1_hat = sb("x1_hat", [P, TT, D], F32)
        h2_full = sb("h2_full", [P, KT, S], F32)
        h2T = [sb(f"h2T_{s}", [P, KT, S], F32R) for s in ("hi", "lo")]
        silu = [sb(f"silu{i}", [P, S], F32) for i in range(2)]
        hid = [sb(f"hid{i}", [P, GROUP, S], F32) for i in range(CT)]
        mag = [sb(f"mag{i}", [P, GROUP, S], F32) for i in range(CT)]
        beats = sb("beats", [P, 6, S], BF16)
        wins = sb("wins", [P, GROUP, S], BF16)
        kept = [[sb(f"kept{c}_{s}", [P, GROUP, S], F32R) for s in ("hi", "lo")] for c in range(CT)]
        y_T = sb("y_T", [P, KT, S], F32)
        y_out = sb("y_out", [P, TT, D], F32)
        ident = sb("ident2", [P, P], F32)
        minus_half = sb("minus_half2", [P, TT], F32)
        mod_ln = sb("mod_ln2", [P, 4], F32)
        gate_now = sb("gate_now2", [P, KT], F32)
        bn = sb("bn2", [P, TT, 6], F32)
        mv = sb("mv2", [P, TT, 2], F32)
        var_eps = sb("var_eps2", [P, TT], F32)
        rstd = sb("rstd2", [P, TT], F32)
        neg_mean = sb("neg_mean2", [P, TT], F32)
        shift = sb("shift2", [P, TT], F32)

        gate_ps = [ps(f"gate_ps{i}") for i in range(2)]
        up_ps = [ps(f"up_ps{i}") for i in range(2)]
        down_ps = [ps(f"down_ps{i}") for i in range(KT)]
        turn_ps = [ps(f"turn_ps{i}") for i in range(KT)]

        stage = [b[:, 2 * i:2 * i + 2, :].rearrange("p a n -> p (a n)") for b in (hid[0], hid[1], mag[1]) for i in range(2)]

        staged = [sem(f"mlp_staged{i}") for i in range(6)]
        stage_hi = sem("mlp_stage_hi")
        weights_ready = sem("mlp_weights_ready")
        down_weights_ready = sem("mlp_down_weights_ready")
        constants = sem("mlp_constants")
        x_loaded = sem("mlp_x_loaded")
        attn_loaded = sem("mlp_attn_loaded")
        turned = sem("mlp_turned")
        x1_ready = sem("mlp_x1_ready")
        stats_steps = sem("mlp_stats_steps")
        stats_ready = sem("mlp_stats_ready")
        norm_steps = sem("mlp_norm_steps")
        x1_normed = sem("mlp_x1_normed")
        mod_picked = sem("mlp_mod_picked")
        h2_full_ready = sem("mlp_h2_full_ready")
        h2_hi = sem("mlp_h2_hi")
        h2_ready = sem("mlp_h2_ready")
        unit_done = sem("mlp_unit_done")
        silu_done = sem("mlp_silu_done")
        hid_ready = sem("mlp_hid_ready")
        mag_ready = sem("mlp_mag_ready")
        rank_steps = sem("mlp_rank_steps")
        kept_full = sem("mlp_kept_full")
        kept_hi = sem("mlp_kept_hi")
        kept_ready = sem("mlp_kept_ready")
        down_summed = sem("mlp_down_summed")
        gate_picked = sem("mlp_gate_picked")
        y_scaled = sem("mlp_y_scaled")
        y_ready = sem("mlp_y_ready")
        stored = sem("mlp_stored")

        loads = [(w_in, w, c) for w_in, w in ((wg_in, wg), (wu_in, wu), (wd_in, wd)) for c in range(2)]

        def part(n, s):
            _, w, c = loads[n]
            return w[s][:, :, :].rearrange("p a n -> p (a n)")[:, c * 1024:(c + 1) * 1024]

        def unit_no(b, c, j):
            return b * UNITS + c * GROUP + j

        def turn_no(b):
            return 2 * KT + (b * 2 * KT if isinstance(b, int) and b < 2 else 2 * 2 * KT + (b - 2) * 3 * KT)

        block = ctx.enter_context(nc.Block())

        @block.sync
        def _(sp):
            sp.dma_start(attn_in[:, :, :], attn_T[0].rearrange("(k p) n -> p k n", p=P)).then_inc(attn_loaded, 16)
            sp.dma_start(x2[:, :, :], x[0].rearrange("(t p) d -> p t d", p=P)).then_inc(x_loaded, 16)
            for n, (w_in, _, c) in enumerate(loads):
                sp.dma_start(stage[n], w_in[:, c * 1024:(c + 1) * 1024]).then_inc(staged[n], 16)

            def load(b):
                sp.wait_ge(x1_ready, KT * b)
                sp.dma_start(x2[:, :, :], x[bass.ds(b, 1)].rearrange("o (t p) d -> p (o t) d", p=P)).then_inc(x_loaded, 16)
                sp.dma_start(attn_in[:, :, :], attn_T[bass.ds(b, 1)].rearrange("o (k p) n -> p (o k) n", p=P))\
                  .then_inc(attn_loaded, 16)

            def store(b):
                sp.wait_ge(y_ready, KT * (b + 1))
                sp.dma_start(out[bass.ds(b, 1)].rearrange("o (t p) d -> p (o t) d", p=P), y_out[:, :, :]).then_inc(stored, 16)

            load(1)
            load(2)
            with sp.Fori(3, B) as b:
                load(b)
                store(b - 3)
            for b in range(B - 3, B):
                store(b)
            sp.wait_ge(stored, 16 * B)

        @block.gpsimd
        def _(pool):
            pool.memset(minus_half[:, :], -0.5).then_inc(constants, 1)
            pool.memset(ident[:, :], 0.0).then_inc(constants, 1)
            pool.wait_ge(constants, 2)
            pool.affine_select(out=ident[:, :], in_=ident[:, :], compare_op=ALU.not_equal, fill=1.0, base=0,
                               pattern=[[-1, P]], channel_multiplier=1).then_inc(constants, 1)

            def layernorm_scale(b):
                wait_alone(pool, stats_ready, b + 1)
                pool.tensor_scalar(var_eps[:, :], mv[:, :, 1], LN_EPS, 1.0, ALU.add, ALU.mult).then_inc(norm_steps, 1)
                pool.tensor_scalar(neg_mean[:, :], mv[:, :, 0], -1.0, 1.0, ALU.mult, ALU.mult).then_inc(norm_steps, 1)
                pool.wait_ge(norm_steps, 4 * b + 2)
                pool.tensor_tensor(rstd[:, :], var_eps[:, :], minus_half[:, :], ALU.pow).then_inc(norm_steps, 1)
                pool.wait_ge(norm_steps, 4 * b + 3)
                pool.tensor_tensor(shift[:, :], neg_mean[:, :], rstd[:, :], ALU.mult).then_inc(norm_steps, 1)

            def kept_lo(b, c):
                for j in range(GROUP):
                    pool.wait_ge(kept_hi, unit_no(b, c, j) + 1)
                    pool.tensor_tensor(kept[c][1][:, j, :], hid[c][:, j, :], kept[c][0][:, j, :].bitcast(F32),
                                       ALU.subtract).then_inc(kept_ready, 1)

            def batch(b, first=False, last=False):
                if not first:
                    kept_lo(b - 1, 1)
                if not last:
                    layernorm_scale(b + 1)
                kept_lo(b, 0)

            layernorm_scale(0)
            for n in range(4, 6):
                pool.wait_ge(stage_hi, n + 1)
                pool.tensor_tensor(part(n, 1), stage[n], part(n, 0).bitcast(F32), ALU.subtract).then_inc(down_weights_ready, 1)
            batch(0, first=True)
            with pool.Fori(1, B - 1) as b:
                batch(b)
            batch(B - 1, last=True)
            kept_lo(B - 1, 1)

        @block.scalar
        def _(act):
            def weight_hi(ns):
                for n in ns:
                    act.wait_ge(staged[n], 16)
                    act.copy(part(n, 0), stage[n]).then_inc(stage_hi, 1)

            def normalize(b):
                act.wait_ge(norm_steps, 4 * b + 4)
                for t in range(TT):
                    act.activation(x1_hat[:, t, :], x1[:, bass.ds(b, 1), t, :].rearrange("p o d -> p (o d)"), ACT.Identity,
                                   bias=shift[:, t:t + 1], scale=rstd[:, t:t + 1]).then_inc(x1_normed, 1)

            def modulate(b, turn):
                act.wait_ge(mod_picked, 2 * b + 2)
                for k in range(KT):
                    act.wait_ge(turned, turn + k + 1)
                    act.activation(h2_full[:, k, :], turn_ps[k][:, :], ACT.Identity, bias=mod_ln[:, 2 + k:3 + k],
                                   scale=mod_ln[:, k:k + 1]).then_inc(h2_full_ready, 1)

            def h_hi(b):
                for k in range(KT):
                    act.wait_ge(h2_full_ready, KT * b + k + 1)
                    act.copy(h2T[0][:, k, :], h2_full[:, k, :]).then_inc(h2_hi, 1)

            def silu_of(b, c, j):
                act.wait_ge(unit_done, unit_no(b, c, j) + 1)
                act.activation(silu[j % 2][:, :], gate_ps[j % 2][:, :], ACT.Silu).then_inc(silu_done, 1)

            def magnitude(b, c, j):
                act.wait_ge(hid_ready, unit_no(b, c, j) + 1)
                act.activation(mag[c][:, j, :], hid[c][:, j, :], ACT.Abs).then_inc(mag_ready, 1)

            def unit(b, c, j):
                silu_of(b, c, j)
                magnitude(b, c, j)

            def kept_his(b, c):
                for j in range(GROUP):
                    act.wait_ge(kept_full, unit_no(b, c, j) + 1)
                    act.copy(kept[c][0][:, j, :], hid[c][:, j, :]).then_inc(kept_hi, 1)

            def scale_y(b, after=True):
                if after:
                    act.wait_ge(y_scaled, KT * b)
                act.copy(gate_now[:, :], mods[:, 2 * GB:2 * GB + 2, bass.ds(b, 1)].rearrange("p m o -> p (m o)"))\
                   .then_inc(gate_picked, 1)
                act.wait_ge(gate_picked, b + 1)
                act.wait_ge(down_summed, b + 1)
                for k in range(KT):
                    act.activation(y_T[:, k, :], down_ps[k][:, :], ACT.Copy, scale=gate_now[:, k:k + 1])\
                       .then_inc(y_scaled, 1)

            def batch(b, first=False, last=False, y_after=True):
                for j in range(GROUP):
                    unit(b, 0, j)
                if not first:
                    kept_his(b - 1, 1)
                if first:
                    act.wait_ge(down_weights_ready, 2)
                silu_of(b, 1, 0)
                if not last:
                    normalize(b + 1)
                magnitude(b, 1, 0)
                unit(b, 1, 1)
                unit(b, 1, 2)
                if not last:
                    modulate(b + 1, turn_no(b + 1) - KT)
                    act.wait_ge(unit_done, unit_no(b, 1, 3) + 1)
                    h_hi(b + 1)
                unit(b, 1, 3)
                if not first:
                    scale_y(b - 1, y_after)
                kept_his(b, 0)

            weight_hi(range(2))
            normalize(0)
            weight_hi(range(2, 4))
            modulate(0, KT)
            h_hi(0)
            weight_hi(range(4, 6))
            batch(0, first=True)
            batch(1, y_after=False)
            with act.Fori(2, B - 1) as b:
                batch(b)
            batch(B - 1, last=True)
            kept_his(B - 1, 1)
            scale_y(B - 1)

        @block.vector
        def _(dve):
            def weight_lo(ns):
                for n in ns:
                    dve.wait_ge(stage_hi, n + 1)
                    dve.tensor_tensor(part(n, 1), stage[n], part(n, 0).bitcast(F32), ALU.subtract)\
                       .then_inc(weights_ready, 1)

            def x1_of(b, rows):
                return x1[:, bass.ds(b, 1), rows, :].rearrange("p o t d -> p (o t) d")

            def residual(b, turn):
                dve.wait_ge(x_loaded, 16 * b + 16)
                for k in range(KT):
                    dve.wait_ge(turned, turn + k + 1)
                    dve.tensor_tensor(x1_of(b, slice(2 * k, 2 * k + 2)), turn_ps[k][:, :].rearrange("p (t d) -> p t d", t=2),
                                      x2[:, 2 * k:2 * k + 2, :], ALU.add).then_inc(x1_ready, 1)

            def statistics(b):
                wait_alone(dve, x1_ready, KT * b + KT)
                for t in range(TT):
                    dve.bn_stats(bn[:, t, :], x1[:, bass.ds(b, 1), t, :].rearrange("p o d -> p (o d)")).then_inc(stats_steps, 1)
                wait_alone(dve, stats_steps, TT * b + TT)
                for t in range(TT):
                    last = dve.bn_aggr(mv[:, t, :], bn[:, t, :])
                last.then_inc(stats_ready, 1)

            def pick_mods(b, after=True):
                if after:
                    dve.wait_ge(h2_full_ready, KT * b)
                dve.tensor_copy(mod_ln[:, 0:2], mods[:, 2 * CB:2 * CB + 2, bass.ds(b, 1)].rearrange("p m o -> p (m o)"))\
                   .then_inc(mod_picked, 1)
                dve.tensor_copy(mod_ln[:, 2:4], mods[:, 2 * SB:2 * SB + 2, bass.ds(b, 1)].rearrange("p m o -> p (m o)"))\
                   .then_inc(mod_picked, 1)

            def h_lo(b):
                for k in range(KT):
                    dve.wait_ge(h2_hi, KT * b + k + 1)
                    dve.tensor_tensor(h2T[1][:, k, :], h2_full[:, k, :], h2T[0][:, k, :].bitcast(F32),
                                      ALU.subtract).then_inc(h2_ready, 1)

            def hidden(b, c, j, reused=True):
                dve.wait_ge(silu_done, unit_no(b, c, j) + 1)
                if reused:
                    dve.wait_ge(kept_ready, unit_no(b - 1, c, j) + 1)
                dve.tensor_tensor(hid[c][:, j, :], up_ps[j % 2][:, :], silu[j % 2][:, :], ALU.mult).then_inc(hid_ready, 1)

            def compare(b, c, i):
                if i == 0:
                    dve.wait_ge(mag_ready, unit_no(b, c, GROUP))
                at, n = (0, 3, 5)[i], GROUP - 1 - i
                dve.tensor_tensor(beats[:, at:at + n, :], mag[c][:, i:i + 1, :].to_broadcast([P, n, S]),
                                  mag[c][:, i + 1:GROUP, :], ALU.is_ge).then_inc(rank_steps, 1)

            def count_wins(b, c):
                steps = 7 * (b * CT + c)
                dve.wait_ge(rank_steps, steps + 3)
                dve.tensor_tensor(wins[:, 0:2, :], beats[:, 0:4:3, :], beats[:, 1:5:3, :], ALU.add).then_inc(rank_steps, 1)
                dve.tensor_tensor(wins[:, 2:4, :], beats[:, 1:3, :], beats[:, 3:5, :], ALU.add).then_inc(rank_steps, 1)
                dve.wait_ge(rank_steps, steps + 5)
                dve.tensor_tensor(wins[:, 0:4:3, :], wins[:, 0:4:3, :], beats[:, 2:6:3, :], ALU.add).then_inc(rank_steps, 1)
                dve.tensor_tensor(wins[:, 1:3, :], wins[:, 1:3, :], beats[:, 0:6:5, :], ALU.subtract).then_inc(rank_steps, 1)

            def keep(b, c):
                dve.wait_ge(rank_steps, 7 * (b * CT + c) + 7)
                for j, (op, at) in enumerate(((ALU.is_ge, 2.0), (ALU.is_ge, 1.0), (ALU.is_le, 0.0), (ALU.is_le, 1.0))):
                    dve.scalar_tensor_tensor(out=hid[c][:, j, :], in0=wins[:, j, :], scalar=at, in1=hid[c][:, j, :],
                                             op0=op, op1=ALU.mult).then_inc(kept_full, 1)

            def rank_part(b, c, part_no):
                if part_no == 0:
                    compare(b, c, 0)
                elif part_no == 1:
                    compare(b, c, 1)
                    compare(b, c, 2)
                elif part_no == 2:
                    count_wins(b, c)
                else:
                    keep(b, c)

            def final(b, turn, stores=True):
                if stores:
                    dve.wait_ge(stored, 16 * b)
                for k in range(KT):
                    dve.wait_ge(turned, turn + k + 1)
                    dve.tensor_tensor(y_out[:, 2 * k:2 * k + 2, :], turn_ps[k][:, :].rearrange("p (t d) -> p t d", t=2),
                                      x1_of(b, slice(2 * k, 2 * k + 2)), ALU.add).then_inc(y_ready, 1)

            def batch(b, first=False, last=False, y=True, stores=True):
                turn = turn_no(b)
                for j in range(GROUP):
                    hidden(b, 0, j, reused=not first)
                    if not first:
                        rank_part(b - 1, 1, j)
                    if j == 0 and y:
                        final(b - 2, turn, stores)
                    if j == 3 and not last:
                        residual(b + 1, turn + (KT if y else 0))
                if not last:
                    statistics(b + 1)
                    pick_mods(b + 1)
                for j in range(GROUP):
                    if j == GROUP - 1 and not last:
                        h_lo(b + 1)
                    hidden(b, 1, j, reused=not first)
                    rank_part(b, 0, j)

            residual(0, 0)
            statistics(0)
            pick_mods(0, after=False)
            weight_lo(range(4))
            h_lo(0)
            batch(0, first=True, y=False)
            batch(1, y=False)
            batch(2, stores=False)
            with dve.Fori(3, B - 1) as b:
                batch(b)
            batch(B - 1, last=True)
            for j in range(GROUP):
                rank_part(B - 1, 1, j)
            turn = turn_no(B - 1) + KT
            final(B - 2, turn)
            final(B - 1, turn + KT)

        @block.tensor
        def _(pe):
            pe.wait_ge(constants, 3)

            def turn_back(src):
                for n in range(KT):
                    for t in range(2):
                        for k in range(KT):
                            mm = pe.transpose(turn_ps[n][:, t * D + k * P:t * D + (k + 1) * P],
                                              src[:, k, (2 * n + t) * P:(2 * n + t + 1) * P], ident[:, :])
                    mm.then_inc(turned, 1)

            def turn_attn(b):
                pe.wait_ge(attn_loaded, 16 * b + 16)
                turn_back(attn_in)

            def turn_y(b):
                pe.wait_ge(y_scaled, KT * b + KT)
                turn_back(y_T)

            def turn_h(b):
                pe.wait_ge(x1_ready, KT * b + KT)
                pe.wait_ge(x1_normed, TT * b + TT)
                for k in range(KT):
                    for t in range(TT):
                        mm = pe.transpose(turn_ps[k][:, t * P:(t + 1) * P], x1_hat[:, t, k * P:(k + 1) * P], ident[:, :])
                    mm.then_inc(turned, 1)

            def gate_up(b, c, j, reused=True):
                if reused:
                    pe.wait_ge(hid_ready, unit_no(b, c, j) - 1)
                cols = slice((c * GROUP + j) * P, (c * GROUP + j + 1) * P)
                for m, (w, bank) in enumerate(((wg, gate_ps[j % 2]), (wu, up_ps[j % 2]))):
                    for k in range(KT):
                        if c == 0 and j == 0 and m == 0:
                            pe.wait_ge(h2_ready, KT * b + k + 1)
                        for n, (l, r) in enumerate(split_passes(w[0][:, k, cols], w[1][:, k, cols],
                                                                h2T[0][:, k, :], h2T[1][:, k, :])):
                            mm = pe.matmul(bank[:, :], l, r, start=(k == 0 and n == 0), stop=(k == KT - 1 and n == 2))
                mm.then_inc(unit_done, 1)

            def down(b, c, j, free=True):
                if c == 0 and j == 0 and free:
                    pe.wait_ge(y_scaled, KT * b)
                pe.wait_ge(kept_ready, unit_no(b, c, j) + 1)
                for k in range(KT):
                    cols = slice(k * P, (k + 1) * P)
                    t = c * GROUP + j
                    for n, (l, r) in enumerate(split_passes(wd[0][:, t, cols], wd[1][:, t, cols],
                                                            kept[c][0][:, j, :], kept[c][1][:, j, :])):
                        mm = pe.matmul(down_ps[k][:, :], l, r, start=(t == 0 and n == 0),
                                       stop=(t == UNITS - 1 and n == 2))
                if t == UNITS - 1:
                    mm.then_inc(down_summed, 1)

            def batch(b, first=False, last=False, y=True, down_free=True):
                for j in range(GROUP):
                    gate_up(b, 0, j, reused=not (first and j < 2))
                    if j > 0 and not first:
                        down(b - 1, 0, j - 1, down_free)
                    if j == 0 and y:
                        pe.wait_ge(h2_full_ready, KT * b + KT)
                        turn_y(b - 2)
                    if j == 2 and not last:
                        if y:
                            pe.wait_ge(y_ready, KT * (b - 1))
                        else:
                            pe.wait_ge(h2_full_ready, KT * b + KT)
                        turn_attn(b + 1)
                gate_up(b, 1, 0)
                if not first:
                    down(b - 1, 0, 3)
                gate_up(b, 1, 1)
                if not first:
                    down(b - 1, 1, 0)
                gate_up(b, 1, 2)
                if not first:
                    down(b - 1, 1, 1)
                if not last:
                    turn_h(b + 1)
                gate_up(b, 1, 3)
                if not first:
                    down(b - 1, 1, 2)
                    down(b - 1, 1, 3)

            turn_attn(0)
            turn_h(0)
            pe.wait_ge(weights_ready, 4)
            batch(0, first=True, y=False)
            pe.wait_ge(down_weights_ready, 2)
            batch(1, y=False, down_free=False)
            batch(2)
            with pe.Fori(3, B - 1) as b:
                batch(b)
            batch(B - 1, last=True)
            for c in range(CT):
                for j in range(GROUP):
                    down(B - 1, c, j)
                    if c == 0 and j == 1:
                        pe.wait_ge(y_ready, KT * (B - 2))
                        turn_y(B - 2)
            pe.wait_ge(y_ready, KT * (B - 1))
            turn_y(B - 1)


def build(nc, x, wqT, wkT, wvT, woT, wg, wu, wd, cT, wmod, out):
    attn_T = nc.dram_tensor("attn_T", (B, D, S), F32, kind="Internal").ap()
    with nc.sbuf_tensor("mods", [P, 12, B + 1], F32) as mods:
        attention_phase(nc, x, cT, wmod, wqT, wkT, wvT, woT, attn_T, mods)
        mlp_phase(nc, x, attn_T, wg, wu, wd, out, mods)


def kernel(**inputs):
    import concourse.bacc as bacc
    from concourse.bass_utils import run_bass_kernel_spmd as run

    def by_partition(w):
        t = w.shape[0] // P
        return w.reshape(t, P, w.shape[1]).transpose(1, 0, 2).reshape(P, t * w.shape[1])

    def grouped(w):
        return w.reshape(w.shape[0], CT, P, GROUP).transpose(0, 1, 3, 2).reshape(w.shape[0], I)

    a = {k: np.asarray(val) for k, val in inputs.items()}
    wd = a["L0_ffn_w_down"].reshape(CT, P, GROUP, D).transpose(1, 0, 2, 3).reshape(P, CT * GROUP * D)
    arrays = {
        "x": a["L0_attn_resid_pre"],
        "wqT": by_partition(a["L0_attn_Wq"].T),
        "wkT": by_partition(a["L0_attn_Wk"].T),
        "wvT": by_partition(a["L0_attn_Wv"].T),
        "woT": by_partition(a["L0_attn_Wo"].T),
        "wg": by_partition(grouped(a["L0_ffn_w_gate"])),
        "wu": by_partition(grouped(a["L0_ffn_w_up"])),
        "wd": wd,
        "cT": a["L0_c"].T.reshape(KT, P, B).transpose(1, 0, 2),
        "wmod": a["L0_wmod"].reshape(KT, P, 6 * D).transpose(1, 0, 2),
    }
    arrays = {k: np.ascontiguousarray(val) for k, val in arrays.items()}
    nc = bacc.Bacc("TRN2", target_bir_lowering=False, num_devices=1)
    args = [nc.dram_tensor(k, val.shape, F32, kind="ExternalInput").ap() for k, val in arrays.items()]
    out = nc.dram_tensor("out", (B, S, D), F32, kind="ExternalOutput").ap()
    build(nc, *args, out)
    r = run(nc, [arrays], core_ids=[0])
    return r.results[0]["out"]
```

```python
import math
from contextlib import ExitStack

import numpy as np

import concourse.bass as bass
from concourse import mybir

F32 = mybir.dt.float32
F32R = mybir.dt.float32r
BF16 = mybir.dt.bfloat16
ACT = mybir.ActivationFunctionType
ALU = mybir.AluOpType

P = 128
B, S, D = 8, 512, 256
H, DH = 16, 128
HD = H * DH
I = 1024
KT = D // P
TT = S // P
GROUP = 4
CT = I // P // GROUP
LN_EPS = 1e-5
CLIP = 1024.0
MASKED = -1e30
SA, CA, GA, SB, CB, GB = range(6)

SLOPE = [float(np.float32((2 ** (-2 ** (-(math.log2(H) - 3)))) ** (h + 1))) for h in range(H)]

AREA = {3: 0, 2: 512, 0: 896, 1: 1024}
BANKS = [[3], [2, 0], [1]]
BANK_COLS = [(0, 512), (512, 1024), (1024, 1280)]
BLOCK_ORDER = [3, 2, 0, 1]
WIDTH = {i: P * (i + 1) for i in range(TT)}
KEY_AREA = {j: AREA[TT - 1 - j] for j in range(TT)}
KEY_BANKS = [[TT - 1 - i for i in blocks] for blocks in BANKS]
TRI = 1280


def wait_alone(eng, semaphore, value):
    eng.wait_ge(semaphore, value)
    eng.nop(nofuse=True)


def split_passes(hi_l, lo_l, hi_r, lo_r):
    return [(hi_l, hi_r), (hi_l, lo_r), (lo_l, hi_r)]


RING = 6


def next_head(h):
    return (h + 1) % H


def previous_head(h):
    return (h - 1) % H


def v_halves(h, last=False):
    if h == H - 1 and last:
        return []
    if h == H - 1:
        return [(("v", H - 2), 0, 0), (("v", H - 1), 0, 2)]
    return [] if h == H - 2 else [(("v", h), h // 2 + 1, 2 * (h % 2))]


def slot_uses(h, first=False, last=False):
    uses = [("s", h, n) for n in range(3)]
    if not first:
        uses.append(("z", previous_head(h)))
    if not (last and h == H - 1):
        uses += [("q", next_head(h)), ("k", next_head(h))]
    if h == H - 2:
        uses += [("ln", 0), ("ln", 1)]
    return uses + [use for use, _, _ in v_halves(h, last)] + [("t", h, n) for n in range(3)]


PRE_USES = [("ln", 0), ("ln", 1), ("q", 0), ("k", 0), ("v", H - 2), ("v", H - 1)] + slot_uses(0, first=True)
USES = sum([slot_uses(h) for h in list(range(1, H)) + [0]], [])
LAST_USES = sum([slot_uses(h, last=True) for h in range(1, H)], []) + [("z", H - 1), ("h2", 0), ("h2", 1)]
PER_BATCH = len(USES)
assert PER_BATCH % RING == 0
PRE_USE = {u: n for n, u in enumerate(PRE_USES)}
USE = {u: n for n, u in enumerate(USES)}
LAST_USE = {u: n for n, u in enumerate(LAST_USES)}
LAST = B - 1
PRE = None


def has_hi(use):
    return use[0] not in ("ln", "h2", "s")


def ring_use(b, key):
    if b is PRE:
        return PRE_USE[key], PRE_USE[key]
    use = (LAST_USE if isinstance(b, int) else USE)[key]
    return len(PRE_USES) + use, len(PRE_USES) + b * PER_BATCH + use


def use_before(b, key):
    return len(PRE_USES) + b * PER_BATCH + USE[key] - PER_BATCH


def hi_count(b, key):
    in_pre = [u for u in PRE_USES if has_hi(u)]
    in_loop = [u for u in USES if has_hi(u)]
    if b is PRE:
        return in_pre.index(key) + 1
    here = [u for u in LAST_USES if has_hi(u)] if isinstance(b, int) else in_loop
    return len(in_pre) + b * len(in_loop) + here.index(key) + 1


def heads_before(b, h):
    if b is PRE:
        return 0
    return b * H + (h if h else H)


def attention_phase(nc, x, cT, wmod, wqT, wkT, wvT, woT, wg, wu, attn_T, mods, shared):
    with ExitStack() as ctx:
        def sb(name, shape, dt):
            return ctx.enter_context(nc.sbuf_tensor(name, shape, dt))

        def sem(name):
            return ctx.enter_context(nc.semaphore(name))

        wq = [sb(f"wq_{s}", [P, KT, HD], F32R) for s in ("hi", "lo")]
        wk = [sb(f"wk_{s}", [P, KT, HD], F32R) for s in ("hi", "lo")]
        wv = shared["wv_gate_up"]
        wo = [sb(f"wo_{s}", [P, H, D], F32R) for s in ("hi", "lo")]
        hT = shared["hT"]
        qT = [sb(f"qT_{s}", [P, S], F32R) for s in ("hi", "lo")]
        kT = [sb(f"kT_{s}", [P, S], F32R) for s in ("hi", "lo")]
        zT = [sb(f"zT_{s}", [P, S], F32R) for s in ("hi", "lo")]
        v = [sb(f"v_{s}", [P, 2, TT, 2 * DH], F32R) for s in ("hi", "lo")]
        pT = [sb(f"pT_{s}", [P, TRI], F32R) for s in ("hi", "lo")]
        probs = sb("probs", [P, TRI], F32)
        key_pos = sb("key_pos", [P, TRI], F32)
        xin, h_full, out_T, out_T_free = shared["xin"], shared["h_full"], shared["out_T"], shared["out_T_free"]
        x1_first = shared["x1_first"]
        ident = sb("ident", [P, P], F32)
        stage = [x1_first[:, :, :].rearrange("p t d -> p (t d)"), sb("stage1", [P, 1024], F32)[:, :]]
        stage += [probs[:, 0:1024], out_T[:, :, :].rearrange("p k n -> p (k n)")]
        MOD_CHUNKS = 3
        mod_stage = [h_full, out_T, h_full]
        c_sb = sb("c_sb", [P, KT, B], F32)
        c_exp = sb("c_exp", [P, KT, B], F32)
        c_silu = sb("c_silu", [P, KT, B], F32)
        mod_sign = sb("mod_sign", [P, 2, B], F32)
        mod_abs = sb("mod_abs", [P, 2, B], F32)
        mod_ln = sb("mod_ln", [P, 4], F32)
        gate_now = sb("gate_now", [P, KT], F32)
        neg_max = sb("neg_max", [P, TT], F32)
        row_sum = sb("row_sum", [P, TT], F32)
        row_inv = sb("row_inv", [P, TT], F32)
        bn = sb("bn", [P, TT, 6], F32)
        mv = sb("mv", [P, TT, 2], F32)
        var_eps = sb("var_eps", [P, TT], F32)
        minus_half = sb("minus_half", [P, TT], F32)
        rstd = sb("rstd", [P, TT], F32)
        neg_mean = sb("neg_mean", [P, TT], F32)
        shift = sb("shift", [P, TT], F32)

        out_ps = [ctx.enter_context(nc.psum_tensor(f"out_ps{i}", [P, S], F32)) for i in range(KT)]
        ring = [ctx.enter_context(nc.psum_tensor(f"ring{i}", [P, 512], F32)) for i in range(RING)]

        staged = [sem(f"staged{i}") for i in range(len(stage))]
        mod_staged = [sem(f"mod_staged{i}") for i in range(MOD_CHUNKS)]
        mods_summed = sem("mods_summed")
        c_loaded = sem("c_loaded")
        stage_hi = sem("stage_hi")
        stage_free = sem("stage_free")
        c_exp_done = sem("c_exp_done")
        c_steps = sem("c_steps")
        c_ready = sem("c_ready")
        mods_steps = sem("mods_steps")
        constants = sem("constants")
        x_loaded = sem("x_loaded")
        stats_steps = sem("stats_steps")
        stats_ready = sem("stats_ready")
        norm_steps = sem("norm_steps")
        x_normed = sem("x_normed")
        mod_picked = sem("mod_picked")
        hT_hi = sem("hT_hi")
        hT_ready = sem("hT_ready")
        ring_filled = sem("ring_filled")
        ring_hi = sem("ring_hi")
        ring_freed = sem("ring_freed")
        max_ready = sem("max_ready")
        exp_done = sem("exp_done")
        inv_ready = sem("inv_ready")
        probs_ready = sem("probs_ready")
        out_summed = sem("out_summed")
        gate_picked = sem("gate_picked")
        out_taken = sem("out_taken")
        attn_loaded = sem("attn_loaded")
        gate_up_staged = [sem(f"gate_up_staged{i}") for i in range(2)]
        gate_up_hi = sem("gate_up_hi")
        gate_up_freed = [sem(f"gate_up_freed{i}") for i in range(2)]

        weights = [(wqT, wq), (wkT, wk), (wvT, wv), (woT, wo)]
        W_ORDER = [(w, c) for w in range(3) for c in (0, 2)] + [(w, c) for w in range(3) for c in (1, 3)] \
            + [(3, c) for c in range(4)]
        FIRST = 6
        CHUNKS = len(W_ORDER)
        IN_SLOT = CHUNKS - 6
        BUFFER = [n % 3 for n in range(FIRST)] + [(n + 3) % 4 for n in range(IN_SLOT - FIRST)] \
            + [(3, 0, 1)[n % 3] for n in range(CHUNKS - IN_SLOT)]
        USED_BEFORE = [max([m for m in range(n) if BUFFER[m] == BUFFER[n]], default=None) for n in range(CHUNKS)]
        ROUND = [BUFFER[:n + 1].count(BUFFER[n]) for n in range(CHUNKS)]

        gate_up_stage = [stage[3], stage[1]]
        gate_up_chunks = [(w, k, 1024 * m) for m, w in enumerate((wg, wu)) for k in range(KT)]

        def gate_up_chunk(n, s):
            _, k, start = gate_up_chunks[n]
            return wv[s][:, k, start:start + 1024]

        def weight_chunk(n, s):
            w, c = W_ORDER[n]
            return weights[w][1][s][:, :, :].rearrange("p a n -> p (a n)")[:, c * 1024:(c + 1) * 1024]

        def ring_as(use, like):
            bank = ring[use % RING]
            return bank[:, :].rearrange("p (t n) -> p t n", t=2) if len(like.shape) == 3 else bank[:, 0:like.shape[1]]

        def slope_scale(h):
            return 1.0 / (math.sqrt(DH) * SLOPE[h])

        block = ctx.enter_context(nc.Block())

        @block.sync
        def _(sp):
            sp.dma_start(c_sb[:, :, :], cT).then_inc(c_loaded, 16)
            sp.dma_start(xin[:, :, :], x[0].rearrange("(t p) d -> p t d", p=P)).then_inc(x_loaded, 16)
            for n, (w, c) in enumerate(W_ORDER):
                if USED_BEFORE[n] is not None:
                    sp.wait_ge(stage_free, USED_BEFORE[n] + 1)
                elif n >= FIRST:
                    sp.wait_ge(mods_summed, MOD_CHUNKS)
                sp.dma_start(stage[BUFFER[n]], weights[w][0][:, c * 1024:(c + 1) * 1024]).then_inc(staged[BUFFER[n]], 16)
                if n < MOD_CHUNKS:
                    if n == 2:
                        sp.wait_ge(mods_summed, 1)
                    sp.dma_start(mod_stage[n][:, :, :], wmod[:, :, n * 512:(n + 1) * 512]).then_inc(mod_staged[n], 16)

            def step(b, load):
                if load:
                    sp.wait_ge(hT_ready, 2 * b + 2)
                    sp.dma_start(xin[:, :, :],
                                 x[bass.ds(b + 1, 1)].rearrange("o (t p) d -> p (o t) d", p=P)).then_inc(x_loaded, 16)
                sp.wait_ge(out_taken, KT * (b + 2))
                sp.dma_start(attn_T[bass.ds(b, 1)].rearrange("o (k p) n -> p (o k) n", p=P),
                             out_T[:, :, :]).then_inc(out_T_free, 16)

            def load_gate_up(n):
                w, k, _ = gate_up_chunks[n]
                sp.dma_start(gate_up_stage[n % 2], w[:, k * 1024:(k + 1) * 1024]).then_inc(gate_up_staged[n % 2], 16)

            with sp.Fori(0, B - 1) as b:
                step(b, True)
            sp.wait_ge(hT_ready, KT * B)
            sp.dma_start(xin[:, :, :], x[0].rearrange("(t p) d -> p t d", p=P)).then_inc(x_loaded, 16)
            sp.wait_ge(out_T_free, 32)
            sp.dma_start(h_full[:, :, :], attn_T[0].rearrange("(k p) n -> p k n", p=P)).then_inc(attn_loaded, 16)
            sp.wait_ge(out_T_free, 16 * B)
            load_gate_up(0)
            load_gate_up(1)
            for n in (2, 3):
                sp.wait_ge(gate_up_freed[n % 2], 1)
                load_gate_up(n)
            sp.wait_ge(out_taken, KT * (B + 1))
            sp.dma_start(attn_T[B - 1].rearrange("(k p) n -> p k n", p=P), out_T[:, :, :]).then_inc(out_T_free, 16)

        @block.gpsimd
        def _(pool):
            pool.memset(row_sum[:, :], 0.0).then_inc(out_T_free, 16)
            pool.memset(minus_half[:, :], -0.5).then_inc(constants, 1)
            pool.memset(ident[:, :], 0.0).then_inc(constants, 1)
            pool.iota(key_pos[:, 0:512], pattern=[[1, 512]], base=0, channel_multiplier=0,
                      allow_small_or_imprecise_dtypes=True).then_inc(constants, 1)
            pool.wait_ge(constants, 3)
            pool.affine_select(out=ident[:, :], in_=ident[:, :], compare_op=ALU.not_equal, fill=1.0, base=0,
                               pattern=[[-1, P]], channel_multiplier=1).then_inc(constants, 1)
            for i in range(TT - 1):
                pool.tensor_copy(key_pos[:, AREA[i]:AREA[i] + WIDTH[i]], key_pos[:, 0:WIDTH[i]]).then_inc(constants, 1)
            pool.wait_ge(constants, 7)
            for i in range(TT):
                diag = key_pos[:, AREA[i] + P * i:AREA[i] + P * (i + 1)]
                pool.affine_select(out=diag, in_=diag, compare_op=ALU.is_ge, fill=MASKED, base=0,
                                   pattern=[[-1, P]], channel_multiplier=1).then_inc(constants, 1)

            def layernorm(count, src=xin):
                wait_alone(pool, stats_ready, count)
                pool.tensor_scalar(var_eps[:, :], mv[:, :, 1], LN_EPS, 1.0, ALU.add, ALU.mult).then_inc(norm_steps, 1)
                pool.tensor_scalar(neg_mean[:, :], mv[:, :, 0], -1.0, 1.0, ALU.mult, ALU.mult).then_inc(norm_steps, 1)
                pool.wait_ge(norm_steps, 4 * count - 2)
                pool.tensor_tensor(rstd[:, :], var_eps[:, :], minus_half[:, :], ALU.pow).then_inc(norm_steps, 1)
                pool.wait_ge(norm_steps, 4 * count - 1)
                pool.tensor_tensor(shift[:, :], neg_mean[:, :], rstd[:, :], ALU.mult).then_inc(norm_steps, 1)
                wait_alone(pool, norm_steps, 4 * count)
                for t in range(TT):
                    pool.tensor_scalar(xin[:, t, :], src[:, t, :], rstd[:, t:t + 1], shift[:, t:t + 1],
                                       ALU.mult, ALU.add).then_inc(x_normed, 1)

            def slot(b, h):
                heads = heads_before(b, h)
                for n, i in enumerate(BLOCK_ORDER):
                    if n in (0, 3):
                        wait_alone(pool, inv_ready, heads * 2 + (1 if n == 0 else 2))
                    blk = probs[:, AREA[i]:AREA[i] + WIDTH[i]]
                    pool.tensor_scalar(blk, blk, row_inv[:, n:n + 1], 1.0, ALU.mult, ALU.mult).then_inc(probs_ready, 1)
                if h == 3 + TT and b is not LAST:
                    layernorm(b + 2)
                if h == H - 2 and b is not LAST:
                    h_lo(b + 2)

            def h_lo(count, ks=range(KT)):
                for k in ks:
                    pool.wait_ge(hT_hi, KT * (count - 1) + k + 1)
                    pool.tensor_tensor(hT[1][:, k, :], h_full[:, k, :], hT[0][:, k, :].bitcast(F32),
                                       ALU.subtract).then_inc(hT_ready, 1)

            def gate_up_lo(n):
                pool.wait_ge(gate_up_hi, n + 1)
                pool.tensor_tensor(gate_up_chunk(n, 1), gate_up_stage[0], gate_up_chunk(n, 0).bitcast(F32), ALU.subtract)\
                    .then_inc(gate_up_freed[0], 1)

            layernorm(1)
            h_lo(1)
            slot(PRE, 0)
            with pool.Fori(0, LAST) as b:
                for h in range(1, H):
                    slot(b, h)
                slot(b, 0)
            for h in range(1, H):
                slot(LAST, h)
                if h == H - 2:
                    gate_up_lo(0)
            layernorm(B + 1, x1_first)
            gate_up_lo(2)
            h_lo(B + 1, [0])

        @block.scalar
        def _(act):
            act.wait_ge(c_loaded, 16)
            act.activation(c_exp[:, :, :], c_sb[:, :, :], ACT.Exp, scale=-1.0).then_inc(c_exp_done, 1)

            def weight_hi(ns):
                for n in ns:
                    act.wait_ge(staged[BUFFER[n]], 16 * ROUND[n])
                    act.copy(weight_chunk(n, 0), stage[BUFFER[n]]).then_inc(stage_hi, 1)

            def hi(b, key, dst, scale=1.0):
                static, count = ring_use(b, key)
                act.wait_ge(ring_filled, count + 1)
                act.activation(dst, ring_as(static, dst), ACT.Copy, scale=scale).then_inc(ring_hi, 1)

            def gate_up_his(n):
                act.wait_ge(gate_up_staged[n % 2], 16 * (n // 2 + 1))
                act.copy(gate_up_chunk(n, 0), gate_up_stage[n % 2]).then_inc(gate_up_hi, 1)

            def h_hi(b, kind="ln", ks=range(KT)):
                for k in ks:
                    act.wait_ge(ring_freed, ring_use(b, (kind, k))[1] + 1)
                    act.copy(hT[0][:, k, :], h_full[:, k, :]).then_inc(hT_hi, 1)

            def slot(b, h):
                heads = heads_before(b, h)
                if b is PRE:
                    weight_hi([IN_SLOT, IN_SLOT + 1])
                for n, i in enumerate(BLOCK_ORDER):
                    blk = probs[:, AREA[i]:AREA[i] + WIDTH[i]]
                    act.wait_ge(max_ready, heads * TT + n + 1)
                    act.activation(blk, blk, ACT.Exp, bias=neg_max[:, i:i + 1], scale=-1.0,
                                   accum_out=row_sum[:, n:n + 1]).then_inc(exp_done, 1)
                    if b is not PRE and n == 2:
                        hi(b, ("z", previous_head(h)), zT[0][:, :])
                last = b is LAST
                if not (last and h == H - 1):
                    hi(b, ("q", next_head(h)), qT[0][:, :], slope_scale(next_head(h)))
                    hi(b, ("k", next_head(h)), kT[0][:, :])
                if h == H - 2 and last:
                    act.wait_ge(ring_filled, ring_use(b, ("v", H - 3))[1] + 1)
                    gate_up_his(0)
                for key, pair, half in v_halves(h, last):
                    hi(b, key, v[0][:, pair % 2, half:half + 2, :])
                if b is PRE:
                    weight_hi([IN_SLOT + 2, IN_SLOT + 3])
                for n, (start, end) in enumerate(BANK_COLS):
                    hi(b, ("t", h, n), pT[0][:, start:end])
                    if h == H - 2 and not last and n < KT:
                        h_hi(b, ks=[n])
                if b is PRE:
                    weight_hi([IN_SLOT + 4, IN_SLOT + 5])

            weight_hi(range(0, 4))
            h_hi(PRE)
            weight_hi(range(4, IN_SLOT))
            hi(PRE, ("q", 0), qT[0][:, :], slope_scale(0))
            hi(PRE, ("k", 0), kT[0][:, :])
            hi(PRE, ("v", H - 2), v[0][:, 0, 0:2, :])
            hi(PRE, ("v", H - 1), v[0][:, 0, 2:4, :])
            slot(PRE, 0)

            def pick_gates(b):
                act.wait_ge(out_taken, KT * (b + 1))
                act.copy(gate_now[:, :], mods[:, 2 * GA:2 * GA + 2, bass.ds(b, 1)]
                         .rearrange("p m o -> p (m o)")).then_inc(gate_picked, 1)

            def take_out(b):
                act.wait_ge(out_summed, b + 1)
                act.wait_ge(out_T_free, 16 * b + 16)
                act.wait_ge(gate_picked, b + 1)
                act.activation(out_T[:, 0, :], out_ps[0][:, :], ACT.Copy, scale=gate_now[:, 0:1]).then_inc(out_taken, 1)
                act.activation(out_T[:, 1, :], out_ps[1][:, :], ACT.Copy, scale=gate_now[:, 1:2]).then_inc(out_taken, 1)

            with act.Fori(0, LAST) as b:
                pick_gates(b)
                for h in range(1, H):
                    slot(b, h)
                slot(b, 0)
                take_out(b)
            pick_gates(LAST)
            for h in range(1, H):
                if h == H - 1:
                    gate_up_his(1)
                slot(LAST, h)
            gate_up_his(2)
            hi(LAST, ("z", H - 1), zT[0][:, :])
            gate_up_his(3)
            h_hi(LAST, "h2")
            act.wait_ge(gate_up_freed[0], 2)
            take_out(LAST)

        @block.vector
        def _(dve):
            dve.wait_ge(c_exp_done, 1)
            dve.tensor_scalar(c_exp[:, :, :], c_exp[:, :, :], 1.0, None, ALU.add).then_inc(c_steps, 1)
            dve.wait_ge(c_steps, 1)
            dve.reciprocal(c_exp[:, :, :], c_exp[:, :, :]).then_inc(c_steps, 1)
            dve.wait_ge(c_steps, 2)
            dve.tensor_tensor(c_silu[:, :, :], c_sb[:, :, :], c_exp[:, :, :], ALU.mult).then_inc(c_ready, 1)

            def weight_lo(ns):
                for n in ns:
                    dve.wait_ge(stage_hi, n + 1)
                    dve.tensor_tensor(weight_chunk(n, 1), stage[BUFFER[n]], weight_chunk(n, 0).bitcast(F32),
                                      ALU.subtract).then_inc(stage_free, 1)

            def statistics(count, tiles=range(TT), src=xin):
                if tiles[0] == 0:
                    dve.wait_ge(x_loaded, 16 * count)
                for t in tiles:
                    dve.bn_stats(bn[:, t, :], src[:, t, :]).then_inc(stats_steps, 1)

            def mean_and_variance(count):
                wait_alone(dve, stats_steps, TT * count)
                for t in range(TT):
                    last = dve.bn_aggr(mv[:, t, :], bn[:, t, :])
                last.then_inc(stats_ready, 1)

            statistics(1)
            mean_and_variance(1)
            weight_lo(range(0, 4))
            dve.wait_ge(mods_summed, MOD_CHUNKS)
            dve.tensor_copy(mods[:, :, :], out_ps[0][:, 0:12 * B].rearrange("p (m b) -> p m b", b=B)).then_inc(out_taken, KT)
            dve.wait_ge(out_taken, KT)
            for k in (CA, CB):
                m = mods[:, 2 * k:2 * k + 2, :]
                dve.tensor_scalar(m, m, 1.0, None, ALU.add).then_inc(mods_steps, 1)
            for n, k in enumerate((GA, GB)):
                m = mods[:, 2 * k:2 * k + 2, :]
                dve.tensor_scalar(mod_sign[:, :, :], m, 0.0, 2.0, ALU.is_ge, ALU.mult).then_inc(mods_steps, 1)
                dve.scalar_tensor_tensor(out=mod_abs[:, :, :], in0=m, scalar=-1.0, in1=m, op0=ALU.mult,
                                         op1=ALU.max).then_inc(mods_steps, 1)
                dve.wait_ge(mods_steps, 4 + 4 * n)
                dve.tensor_scalar(mod_abs[:, :, :], mod_abs[:, :, :], 0.25, None, ALU.max).then_inc(mods_steps, 1)
                dve.wait_ge(mods_steps, 5 + 4 * n)
                dve.scalar_tensor_tensor(out=m, in0=mod_sign[:, :, :], scalar=-1.0, in1=mod_abs[:, :, :],
                                         op0=ALU.add, op1=ALU.mult).then_inc(mods_steps, 1)
                dve.wait_ge(mods_steps, 6 + 4 * n)

            def gate_up_lo(n):
                dve.wait_ge(gate_up_hi, n + 1)
                dve.tensor_tensor(gate_up_chunk(n, 1), gate_up_stage[1], gate_up_chunk(n, 0).bitcast(F32), ALU.subtract)\
                   .then_inc(gate_up_freed[1], 1)

            def first_residual():
                dve.wait_ge(x_loaded, 16 * (B + 1))
                for n in range(KT):
                    static, number = ring_use(LAST, ("ln", n))
                    dve.wait_ge(ring_filled, number + 1)
                    dve.tensor_tensor(x1_first[:, 2 * n:2 * n + 2, :], ring[static % RING][:, :].rearrange("p (t d) -> p t d", t=2),
                                      xin[:, 2 * n:2 * n + 2, :], ALU.add).then_inc(ring_freed, 1)

            def modulate(b, batch, count, kind="ln", factor=CA, shift_by=SA):
                dve.tensor_copy(mod_ln[:, 0:2], mods[:, 2 * factor:2 * factor + 2, batch].rearrange("p m o -> p (m o)"))\
                   .then_inc(mod_picked, 1)
                dve.tensor_copy(mod_ln[:, 2:4], mods[:, 2 * shift_by:2 * shift_by + 2, batch].rearrange("p m o -> p (m o)"))\
                   .then_inc(mod_picked, 1)
                dve.wait_ge(mod_picked, 2 * count)
                for k in range(KT):
                    static, number = ring_use(b, (kind, k))
                    dve.wait_ge(ring_filled, number + 1)
                    dve.tensor_scalar(h_full[:, k, :], ring[static % RING][:, :], mod_ln[:, k:k + 1],
                                      mod_ln[:, 2 + k:3 + k], ALU.mult, ALU.add).then_inc(ring_freed, 1)

            def lo(b, key, parts, scale=None):
                static = ring_use(b, key)[0]
                dve.wait_ge(ring_hi, hi_count(b, key))
                if scale is None:
                    dve.tensor_tensor(parts[1], ring_as(static, parts[1]), parts[0].bitcast(F32),
                                      ALU.subtract).then_inc(ring_freed, 1)
                else:
                    dve.scalar_tensor_tensor(out=parts[1], in0=ring_as(static, parts[1]), scalar=scale,
                                             in1=parts[0].bitcast(F32), op0=ALU.mult,
                                             op1=ALU.subtract).then_inc(ring_freed, 1)

            def slot(b, h):
                heads = heads_before(b, h)
                limit = CLIP / SLOPE[h]
                for n, (start, end) in enumerate(BANK_COLS):
                    static, number = ring_use(b, ("s", h, n))
                    dve.wait_ge(ring_filled, number + 1)
                    dve.tensor_scalar(probs[:, start:end], ring[static % RING][:, 0:end - start],
                                      limit, -limit, ALU.min, ALU.max).then_inc(ring_freed, 1)
                    wait_alone(dve, ring_freed, number + 1)
                    for i in BANKS[n]:
                        blk = probs[:, AREA[i]:AREA[i] + WIDTH[i]]
                        dve.tensor_tensor_reduce(blk, blk, key_pos[:, AREA[i]:AREA[i] + WIDTH[i]], -SLOPE[h], 3e38,
                                                 ALU.add, ALU.min, neg_max[:, i:i + 1]).then_inc(max_ready, 1)
                if b is PRE:
                    weight_lo([IN_SLOT, IN_SLOT + 1])
                dve.wait_ge(exp_done, heads * TT + 3)
                dve.reciprocal(row_inv[:, 0:3], row_sum[:, 0:3]).then_inc(inv_ready, 1)
                if b is not PRE:
                    lo(b, ("z", previous_head(h)), [t[:, :] for t in zT])
                dve.wait_ge(exp_done, heads * TT + TT)
                dve.reciprocal(row_inv[:, 3:4], row_sum[:, 3:4]).then_inc(inv_ready, 1)
                last = b is LAST
                if not (last and h == H - 1):
                    lo(b, ("q", next_head(h)), [t[:, :] for t in qT], slope_scale(next_head(h)))
                    lo(b, ("k", next_head(h)), [t[:, :] for t in kT])
                if h == H - 2 and not last:
                    modulate(b, bass.ds(b + 1, 1), b + 2)
                if h == H - 2 and last:
                    first_residual()
                if h == H - 1 and last:
                    dve.wait_ge(ring_freed, ring_use(LAST, ("ln", 1))[1] + 1)
                    statistics(B + 1, src=x1_first)
                    mean_and_variance(B + 1)
                    gate_up_lo(1)
                for key, pair, half in v_halves(h, last):
                    lo(b, key, [t[:, pair % 2, half:half + 2, :] for t in v])
                if b is PRE:
                    weight_lo([IN_SLOT + 2, IN_SLOT + 3])
                for n, (start, end) in enumerate(BANK_COLS):
                    lo(b, ("t", h, n), [t[:, start:end] for t in pT])
                if b is PRE:
                    weight_lo([IN_SLOT + 4, IN_SLOT + 5])
                if 3 <= h < 3 + TT and not last:
                    statistics(b + 2, [h - 3])
                if h == 3 + TT and not last:
                    mean_and_variance(b + 2)

            modulate(PRE, slice(0, 1), 1)
            weight_lo(range(4, IN_SLOT))
            lo(PRE, ("q", 0), [t[:, :] for t in qT], slope_scale(0))
            lo(PRE, ("k", 0), [t[:, :] for t in kT])
            lo(PRE, ("v", H - 2), [t[:, 0, 0:2, :] for t in v])
            lo(PRE, ("v", H - 1), [t[:, 0, 2:4, :] for t in v])
            dve.wait_ge(constants, 11)
            slot(PRE, 0)
            with dve.Fori(0, LAST) as b:
                for h in range(1, H):
                    slot(b, h)
                slot(b, 0)
            for h in range(1, H):
                slot(LAST, h)
            lo(LAST, ("z", H - 1), [t[:, :] for t in zT])
            modulate(LAST, slice(0, 1), B + 1, "h2", CB, SB)
            gate_up_lo(3)
            dve.wait_ge(hT_hi, KT * (B + 1))
            dve.tensor_tensor(hT[1][:, 1, :], h_full[:, 1, :], hT[0][:, 1, :].bitcast(F32), ALU.subtract).then_inc(hT_ready, 1)

        @block.tensor
        def _(pe):
            pe.wait_ge(constants, 4)
            for n in range(MOD_CHUNKS):
                pe.wait_ge(mod_staged[n], 16)
                if n == 0:
                    pe.wait_ge(c_ready, 1)
                w = mod_stage[n]
                for t in range(4):
                    m = 4 * n + t
                    for k in range(KT):
                        mm = pe.matmul(out_ps[0][:, m * B:(m + 1) * B], w[:, k, t * P:(t + 1) * P], c_silu[:, k, :],
                                       start=(k == 0), stop=(k == KT - 1))
                mm.then_inc(mods_summed, 1)

            def accumulate(out, terms):
                for n, (l, r) in enumerate(terms):
                    mm = pe.matmul(out, l, r, start=(n == 0), stop=(n == len(terms) - 1))
                return mm

            def claim(b, key):
                static, number = ring_use(b, key)
                if not (b is PRE and number < RING):
                    pe.wait_ge(ring_freed, number - RING + 1)
                return ring[static % RING]

            def turn_first_attention():
                pe.wait_ge(attn_loaded, 16)
                for n in range(KT):
                    bank = claim(LAST, ("ln", n))
                    for t in range(2):
                        for k in range(KT):
                            mm = pe.transpose(bank[:, t * D + k * P:t * D + (k + 1) * P],
                                              h_full[:, k, (2 * n + t) * P:(2 * n + t + 1) * P], ident[:, :])
                    mm.then_inc(ring_filled, 1)

            def turn_x(b, ln_count, kind="ln"):
                for k in range(KT):
                    bank = claim(b, (kind, k))
                    for t in range(TT):
                        if k == 0:
                            pe.wait_ge(x_normed, TT * (ln_count - 1) + t + 1)
                        mm = pe.transpose(bank[:, t * P:(t + 1) * P], xin[:, t, k * P:(k + 1) * P], ident[:, :])
                    mm.then_inc(ring_filled, 1)

            def project(b, kind, w, h):
                bank = claim(b, (kind, h))
                cols = slice(h * DH, (h + 1) * DH)
                terms = []
                for k in range(KT):
                    terms += split_passes(w[0][:, k, cols], w[1][:, k, cols], hT[0][:, k, :], hT[1][:, k, :])
                accumulate(bank[:, :], terms).then_inc(ring_filled, 1)

            def project_v(b, key, pair, half):
                bank = claim(b, key)
                cols = slice(pair * 2 * DH, (pair + 1) * 2 * DH)
                for t in range(2):
                    rows = slice((half + t) * P, (half + t + 1) * P)
                    terms = []
                    for k in range(KT):
                        terms += split_passes(hT[0][:, k, rows], hT[1][:, k, rows], wv[0][:, k, cols], wv[1][:, k, cols])
                    mm = accumulate(bank[:, t * 256:(t + 1) * 256], terms)
                mm.then_inc(ring_filled, 1)

            def scores(b, h):
                number = use_before(b, ("k", h)) if h == 1 else ring_use(b, ("k", h))[1]
                pe.wait_ge(ring_freed, number + 1)
                for n, blocks in enumerate(BANKS):
                    bank = claim(b, ("s", h, n))
                    for i in blocks:
                        rows = slice(i * P, (i + 1) * P)
                        cols = slice(AREA[i] - BANK_COLS[n][0], AREA[i] - BANK_COLS[n][0] + WIDTH[i])
                        mm = accumulate(bank[:, cols], split_passes(qT[0][:, rows], qT[1][:, rows],
                                                                    kT[0][:, 0:WIDTH[i]], kT[1][:, 0:WIDTH[i]]))
                    mm.then_inc(ring_filled, 1)

            def turn_probs(b, h):
                pe.wait_ge(probs_ready, heads_before(b, h) * TT + TT)
                for n, keys in enumerate(KEY_BANKS):
                    bank = claim(b, ("t", h, n))
                    for j in keys:
                        for i in range(j, TT):
                            col = KEY_AREA[j] - BANK_COLS[n][0] + (i - j) * P
                            mm = pe.transpose(bank[:, col:col + P], probs[:, AREA[i] + j * P:AREA[i] + (j + 1) * P],
                                              ident[:, :])
                    mm.then_inc(ring_filled, 1)

            def attend(b, h):
                bank = claim(b, ("z", h))
                for m, keys in enumerate(KEY_BANKS):
                    number = use_before(b, ("t", h, m)) if h == 0 else ring_use(b, ("t", h, m))[1]
                    pe.wait_ge(ring_freed, number + 1)
                    for j in keys:
                        cols = slice(KEY_AREA[j], KEY_AREA[j] + S - j * P)
                        vj = [t[:, (h // 2) % 2, j, (h % 2) * DH:(h % 2 + 1) * DH] for t in v]
                        for n, (l, r) in enumerate(split_passes(vj[0], vj[1], pT[0][:, cols], pT[1][:, cols])):
                            mm = pe.matmul(bank[:, j * P:S], l, r, start=(j == 0 and n == 0),
                                           stop=(j == KEY_BANKS[-1][-1] and n == 2))
                mm.then_inc(ring_filled, 1)

            def project_out(b, h):
                pe.wait_ge(ring_freed, ring_use(b, ("z", h))[1] + 1)
                if h == 0:
                    pe.wait_ge(out_taken, KT * (b + 1))
                    pe.wait_ge(stage_free, CHUNKS)
                for k in range(KT):
                    cols = slice(k * P, (k + 1) * P)
                    terms = split_passes(wo[0][:, h, cols], wo[1][:, h, cols], zT[0][:, :], zT[1][:, :])
                    for n, (l, r) in enumerate(terms):
                        mm = pe.matmul(out_ps[k][:, :], l, r, start=(h == 0 and n == 0),
                                       stop=(h == H - 1 and n == 2))
                if h == H - 1:
                    mm.then_inc(out_summed, 1)

            def slot(b, h):
                scores(b, h)
                if b is not PRE:
                    attend(b, previous_head(h))
                last = b is LAST
                if h == H - 1 and not last:
                    pe.wait_ge(hT_ready, KT * (b + 2))
                if not (last and h == H - 1):
                    project(b, "q", wq, next_head(h))
                    project(b, "k", wk, next_head(h))
                if h == H - 2 and not last:
                    turn_x(b, b + 2)
                if h == H - 2 and last:
                    turn_first_attention()
                for key, pair, half in v_halves(h, last):
                    project_v(b, key, pair, half)
                if b is not PRE:
                    project_out(b, previous_head(h))
                turn_probs(b, h)

            turn_x(PRE, 1)
            pe.wait_ge(stage_free, FIRST)
            pe.wait_ge(hT_ready, KT)
            project(PRE, "q", wq, 0)
            project(PRE, "k", wk, 0)
            project_v(PRE, ("v", H - 2), 0, 0)
            project_v(PRE, ("v", H - 1), 0, 2)
            slot(PRE, 0)
            with pe.Fori(0, LAST) as b:
                for h in range(1, H):
                    slot(b, h)
                slot(b, 0)
            for h in range(1, H):
                slot(LAST, h)
            attend(LAST, H - 1)
            turn_x(LAST, B + 1, "h2")
            project_out(LAST, H - 1)


def mlp_phase(nc, x, attn_T, wd_in, out, mods, shared):
    UNITS = CT * GROUP
    with ExitStack() as ctx:
        def sb(name, shape, dt):
            return ctx.enter_context(nc.sbuf_tensor(name, shape, dt))

        def sem(name):
            return ctx.enter_context(nc.semaphore(name))

        def ps(name):
            return ctx.enter_context(nc.psum_tensor(name, [P, 512], F32))

        wg = [t[:, :, 0:I] for t in shared["wv_gate_up"]]
        wu = [t[:, :, I:2 * I] for t in shared["wv_gate_up"]]
        wd = [sb(f"wd_{s}", [P, UNITS, D], F32R) for s in ("hi", "lo")]
        x2 = sb("x2", [P, TT, D], F32)
        attn_in = sb("attn_in", [P, KT, S], F32)
        x1 = sb("x1", [P, B - 1, TT, D], F32)
        x1_first = shared["x1_first"]
        x1_hat, h2_full, h2T = shared["xin"], shared["h_full"], shared["hT"]
        silu = [sb(f"silu{i}", [P, S], F32) for i in range(2)]
        hid = [sb(f"hid{i}", [P, GROUP, S], F32) for i in range(CT)]
        mag = [sb(f"mag{i}", [P, GROUP, S], F32) for i in range(CT)]
        beats = sb("beats", [P, 6, S], BF16)
        wins = sb("wins", [P, GROUP, S], BF16)
        kept = [[sb(f"kept{c}_{s}", [P, GROUP, S], F32R) for s in ("hi", "lo")] for c in range(CT)]
        y_T = shared["out_T"]
        y_out = sb("y_out", [P, TT, D], F32)
        ident = sb("ident2", [P, P], F32)
        minus_half = sb("minus_half2", [P, TT], F32)
        mod_ln = sb("mod_ln2", [P, 4], F32)
        gate_now = sb("gate_now2", [P, KT], F32)
        bn = sb("bn2", [P, TT, 6], F32)
        mv = sb("mv2", [P, TT, 2], F32)
        var_eps = sb("var_eps2", [P, TT], F32)
        rstd = sb("rstd2", [P, TT], F32)
        neg_mean = sb("neg_mean2", [P, TT], F32)
        shift = sb("shift2", [P, TT], F32)

        gate_ps = [ps(f"gate_ps{i}") for i in range(2)]
        up_ps = [ps(f"up_ps{i}") for i in range(2)]
        down_ps = [ps(f"down_ps{i}") for i in range(KT)]
        turn_ps = [ps(f"turn_ps{i}") for i in range(KT)]

        stage = [mag[1][:, 2 * i:2 * i + 2, :].rearrange("p a n -> p (a n)") for i in range(2)]

        staged = [sem(f"mlp_staged{i}") for i in range(2)]
        stage_hi = sem("mlp_stage_hi")
        down_weights_ready = sem("mlp_down_weights_ready")
        constants = sem("mlp_constants")
        x_loaded = sem("mlp_x_loaded")
        attn_loaded = sem("mlp_attn_loaded")
        turned = sem("mlp_turned")
        x1_ready = sem("mlp_x1_ready")
        stats_steps = sem("mlp_stats_steps")
        stats_ready = sem("mlp_stats_ready")
        norm_steps = sem("mlp_norm_steps")
        x1_normed = sem("mlp_x1_normed")
        mod_picked = sem("mlp_mod_picked")
        h2_full_ready = sem("mlp_h2_full_ready")
        h2_hi = sem("mlp_h2_hi")
        h2_ready = sem("mlp_h2_ready")
        unit_done = sem("mlp_unit_done")
        silu_done = sem("mlp_silu_done")
        hid_ready = sem("mlp_hid_ready")
        mag_ready = sem("mlp_mag_ready")
        rank_steps = sem("mlp_rank_steps")
        kept_full = sem("mlp_kept_full")
        kept_hi = sem("mlp_kept_hi")
        kept_ready = sem("mlp_kept_ready")
        down_summed = sem("mlp_down_summed")
        gate_picked = sem("mlp_gate_picked")
        y_scaled = sem("mlp_y_scaled")
        y_ready = sem("mlp_y_ready")
        stored = sem("mlp_stored")

        def part(n, s):
            return wd[s][:, :, :].rearrange("p a n -> p (a n)")[:, n * 1024:(n + 1) * 1024]

        def unit_no(b, c, j):
            return b * UNITS + c * GROUP + j

        def turn_no(b):
            return b * 2 * KT if isinstance(b, int) and b < 2 else 2 * 2 * KT + (b - 2) * 3 * KT

        out_T_free = shared["out_T_free"]
        block = ctx.enter_context(nc.Block())

        @block.sync
        def _(sp):
            def load(b, after=True):
                if after:
                    sp.wait_ge(x1_ready, KT * (b - 1))
                sp.dma_start(x2[:, :, :], x[bass.ds(b, 1)].rearrange("o (t p) d -> p (o t) d", p=P)).then_inc(x_loaded, 16)
                sp.dma_start(attn_in[:, :, :], attn_T[bass.ds(b, 1)].rearrange("o (k p) n -> p (o k) n", p=P))\
                  .then_inc(attn_loaded, 16)

            def store(b):
                sp.wait_ge(y_ready, KT * (b + 1))
                sp.dma_start(out[bass.ds(b, 1)].rearrange("o (t p) d -> p (o t) d", p=P), y_out[:, :, :]).then_inc(stored, 16)

            load(1, after=False)
            for n in range(2):
                sp.dma_start(stage[n], wd_in[:, n * 1024:(n + 1) * 1024]).then_inc(staged[n], 16)
            load(2)
            sp.wait_ge(out_T_free, 16 * (B + 1))
            with sp.Fori(3, B) as b:
                load(b)
                store(b - 3)
            for b in range(B - 3, B):
                store(b)
            sp.wait_ge(stored, 16 * B)

        @block.gpsimd
        def _(pool):
            pool.memset(minus_half[:, :], -0.5).then_inc(constants, 1)
            pool.memset(ident[:, :], 0.0).then_inc(constants, 1)
            pool.wait_ge(constants, 2)
            pool.affine_select(out=ident[:, :], in_=ident[:, :], compare_op=ALU.not_equal, fill=1.0, base=0,
                               pattern=[[-1, P]], channel_multiplier=1).then_inc(constants, 1)

            def layernorm_scale(b):
                wait_alone(pool, stats_ready, b)
                pool.tensor_scalar(var_eps[:, :], mv[:, :, 1], LN_EPS, 1.0, ALU.add, ALU.mult).then_inc(norm_steps, 1)
                pool.tensor_scalar(neg_mean[:, :], mv[:, :, 0], -1.0, 1.0, ALU.mult, ALU.mult).then_inc(norm_steps, 1)
                pool.wait_ge(norm_steps, 4 * b - 2)
                pool.tensor_tensor(rstd[:, :], var_eps[:, :], minus_half[:, :], ALU.pow).then_inc(norm_steps, 1)
                pool.wait_ge(norm_steps, 4 * b - 1)
                pool.tensor_tensor(shift[:, :], neg_mean[:, :], rstd[:, :], ALU.mult).then_inc(norm_steps, 1)

            def kept_lo(b, c):
                for j in range(GROUP):
                    pool.wait_ge(kept_hi, unit_no(b, c, j) + 1)
                    pool.tensor_tensor(kept[c][1][:, j, :], hid[c][:, j, :], kept[c][0][:, j, :].bitcast(F32),
                                       ALU.subtract).then_inc(kept_ready, 1)

            def batch(b, first=False, last=False):
                if not first:
                    kept_lo(b - 1, 1)
                if not last:
                    layernorm_scale(b + 1)
                kept_lo(b, 0)

            for n in range(2):
                pool.wait_ge(stage_hi, n + 1)
                pool.tensor_tensor(part(n, 1), stage[n], part(n, 0).bitcast(F32), ALU.subtract).then_inc(down_weights_ready, 1)
            batch(0, first=True)
            with pool.Fori(1, B - 1) as b:
                batch(b)
            batch(B - 1, last=True)
            kept_lo(B - 1, 1)

        @block.scalar
        def _(act):
            def weight_hi(ns):
                for n in ns:
                    act.wait_ge(staged[n], 16)
                    act.copy(part(n, 0), stage[n]).then_inc(stage_hi, 1)

            def normalize(b):
                act.wait_ge(norm_steps, 4 * b)
                for t in range(TT):
                    act.activation(x1_hat[:, t, :], x1[:, bass.ds(b - 1, 1), t, :].rearrange("p o d -> p (o d)"), ACT.Identity,
                                   bias=shift[:, t:t + 1], scale=rstd[:, t:t + 1]).then_inc(x1_normed, 1)

            def modulate(b, turn):
                act.wait_ge(mod_picked, 2 * b)
                for k in range(KT):
                    act.wait_ge(turned, turn + k + 1)
                    act.activation(h2_full[:, k, :], turn_ps[k][:, :], ACT.Identity, bias=mod_ln[:, 2 + k:3 + k],
                                   scale=mod_ln[:, k:k + 1]).then_inc(h2_full_ready, 1)

            def h_hi(b):
                for k in range(KT):
                    act.wait_ge(h2_full_ready, KT * (b - 1) + k + 1)
                    act.copy(h2T[0][:, k, :], h2_full[:, k, :]).then_inc(h2_hi, 1)

            def silu_of(b, c, j):
                act.wait_ge(unit_done, unit_no(b, c, j) + 1)
                act.activation(silu[j % 2][:, :], gate_ps[j % 2][:, :], ACT.Silu).then_inc(silu_done, 1)

            def magnitude(b, c, j):
                act.wait_ge(hid_ready, unit_no(b, c, j) + 1)
                act.activation(mag[c][:, j, :], hid[c][:, j, :], ACT.Abs).then_inc(mag_ready, 1)

            def unit(b, c, j):
                silu_of(b, c, j)
                magnitude(b, c, j)

            def kept_his(b, c):
                for j in range(GROUP):
                    act.wait_ge(kept_full, unit_no(b, c, j) + 1)
                    act.copy(kept[c][0][:, j, :], hid[c][:, j, :]).then_inc(kept_hi, 1)

            def scale_y(b, after=True):
                if after:
                    act.wait_ge(y_scaled, KT * b)
                act.copy(gate_now[:, :], mods[:, 2 * GB:2 * GB + 2, bass.ds(b, 1)].rearrange("p m o -> p (m o)"))\
                   .then_inc(gate_picked, 1)
                act.wait_ge(gate_picked, b + 1)
                act.wait_ge(down_summed, b + 1)
                for k in range(KT):
                    act.activation(y_T[:, k, :], down_ps[k][:, :], ACT.Copy, scale=gate_now[:, k:k + 1])\
                       .then_inc(y_scaled, 1)

            def batch(b, first=False, last=False, y_after=True):
                for j in range(GROUP):
                    unit(b, 0, j)
                    if first and j == 1:
                        weight_hi(range(2))
                if not first:
                    kept_his(b - 1, 1)
                if first:
                    act.wait_ge(down_weights_ready, 2)
                silu_of(b, 1, 0)
                if not last:
                    normalize(b + 1)
                magnitude(b, 1, 0)
                unit(b, 1, 1)
                if first:
                    modulate(b + 1, turn_no(b + 1) - KT)
                unit(b, 1, 2)
                if not last and not first:
                    modulate(b + 1, turn_no(b + 1) - KT)
                if not last:
                    act.wait_ge(unit_done, unit_no(b, 1, 3) + 1)
                    h_hi(b + 1)
                unit(b, 1, 3)
                if last:
                    kept_his(b, 0)
                if not first:
                    scale_y(b - 1, y_after)
                if not last:
                    kept_his(b, 0)

            batch(0, first=True)
            act.wait_ge(out_T_free, 16 * (B + 1))
            batch(1, y_after=False)
            with act.Fori(2, B - 1) as b:
                batch(b)
            batch(B - 1, last=True)
            kept_his(B - 1, 1)
            scale_y(B - 1)

        @block.vector
        def _(dve):
            def x1_of(b, rows):
                if isinstance(b, int) and b == 0:
                    return x1_first[:, rows, :]
                return x1[:, bass.ds(b - 1, 1), rows, :].rearrange("p o t d -> p (o t) d")

            def residual(b, turn):
                dve.wait_ge(x_loaded, 16 * b)
                for k in range(KT):
                    dve.wait_ge(turned, turn + k + 1)
                    dve.tensor_tensor(x1_of(b, slice(2 * k, 2 * k + 2)), turn_ps[k][:, :].rearrange("p (t d) -> p t d", t=2),
                                      x2[:, 2 * k:2 * k + 2, :], ALU.add).then_inc(x1_ready, 1)

            def statistics(b):
                wait_alone(dve, x1_ready, KT * b)
                for t in range(TT):
                    dve.bn_stats(bn[:, t, :], x1[:, bass.ds(b - 1, 1), t, :].rearrange("p o d -> p (o d)")).then_inc(stats_steps, 1)
                wait_alone(dve, stats_steps, TT * b)
                for t in range(TT):
                    last = dve.bn_aggr(mv[:, t, :], bn[:, t, :])
                last.then_inc(stats_ready, 1)

            def pick_mods(b, after=True):
                if after:
                    dve.wait_ge(h2_full_ready, KT * (b - 1))
                dve.tensor_copy(mod_ln[:, 0:2], mods[:, 2 * CB:2 * CB + 2, bass.ds(b, 1)].rearrange("p m o -> p (m o)"))\
                   .then_inc(mod_picked, 1)
                dve.tensor_copy(mod_ln[:, 2:4], mods[:, 2 * SB:2 * SB + 2, bass.ds(b, 1)].rearrange("p m o -> p (m o)"))\
                   .then_inc(mod_picked, 1)

            def h_lo(b):
                for k in range(KT):
                    dve.wait_ge(h2_hi, KT * (b - 1) + k + 1)
                    dve.tensor_tensor(h2T[1][:, k, :], h2_full[:, k, :], h2T[0][:, k, :].bitcast(F32),
                                      ALU.subtract).then_inc(h2_ready, 1)

            def hidden(b, c, j, reused=True):
                dve.wait_ge(silu_done, unit_no(b, c, j) + 1)
                if reused:
                    dve.wait_ge(kept_ready, unit_no(b - 1, c, j) + 1)
                dve.tensor_tensor(hid[c][:, j, :], up_ps[j % 2][:, :], silu[j % 2][:, :], ALU.mult).then_inc(hid_ready, 1)

            def compare(b, c, i):
                if i == 0:
                    dve.wait_ge(mag_ready, unit_no(b, c, GROUP))
                at, n = (0, 3, 5)[i], GROUP - 1 - i
                dve.tensor_tensor(beats[:, at:at + n, :], mag[c][:, i:i + 1, :].to_broadcast([P, n, S]),
                                  mag[c][:, i + 1:GROUP, :], ALU.is_ge).then_inc(rank_steps, 1)

            def count_wins(b, c):
                steps = 7 * (b * CT + c)
                dve.wait_ge(rank_steps, steps + 3)
                dve.tensor_tensor(wins[:, 0:2, :], beats[:, 0:4:3, :], beats[:, 1:5:3, :], ALU.add).then_inc(rank_steps, 1)
                dve.tensor_tensor(wins[:, 2:4, :], beats[:, 1:3, :], beats[:, 3:5, :], ALU.add).then_inc(rank_steps, 1)
                dve.wait_ge(rank_steps, steps + 5)
                dve.tensor_tensor(wins[:, 0:4:3, :], wins[:, 0:4:3, :], beats[:, 2:6:3, :], ALU.add).then_inc(rank_steps, 1)
                dve.tensor_tensor(wins[:, 1:3, :], wins[:, 1:3, :], beats[:, 0:6:5, :], ALU.subtract).then_inc(rank_steps, 1)

            def keep(b, c):
                dve.wait_ge(rank_steps, 7 * (b * CT + c) + 7)
                for j, (op, at) in enumerate(((ALU.is_ge, 2.0), (ALU.is_ge, 1.0), (ALU.is_le, 0.0), (ALU.is_le, 1.0))):
                    dve.scalar_tensor_tensor(out=hid[c][:, j, :], in0=wins[:, j, :], scalar=at, in1=hid[c][:, j, :],
                                             op0=op, op1=ALU.mult).then_inc(kept_full, 1)

            def rank_part(b, c, part_no):
                if part_no == 0:
                    compare(b, c, 0)
                elif part_no == 1:
                    compare(b, c, 1)
                    compare(b, c, 2)
                elif part_no == 2:
                    count_wins(b, c)
                else:
                    keep(b, c)

            def final(b, turn, stores=True):
                if stores:
                    dve.wait_ge(stored, 16 * b)
                for k in range(KT):
                    dve.wait_ge(turned, turn + k + 1)
                    dve.tensor_tensor(y_out[:, 2 * k:2 * k + 2, :], turn_ps[k][:, :].rearrange("p (t d) -> p t d", t=2),
                                      x1_of(b, slice(2 * k, 2 * k + 2)), ALU.add).then_inc(y_ready, 1)

            def batch(b, first=False, last=False, y=True, stores=True):
                turn = turn_no(b)
                for j in range(GROUP):
                    hidden(b, 0, j, reused=not first)
                    if not first:
                        rank_part(b - 1, 1, j)
                    if j == 0 and y:
                        final(b - 2, turn, stores)
                    if j == (2 if first else 3) and not last:
                        residual(b + 1, turn + (KT if y else 0))
                if not last:
                    statistics(b + 1)
                    pick_mods(b + 1, after=not first)
                for j in range(GROUP):
                    if j == GROUP - 1 and not last and not first:
                        h_lo(b + 1)
                    hidden(b, 1, j, reused=not first)
                    if j == GROUP - 2 and first:
                        h_lo(b + 1)
                    rank_part(b, 0, j)

            batch(0, first=True, y=False)
            batch(1, y=False)
            batch(2, stores=False)
            with dve.Fori(3, B - 1) as b:
                batch(b)
            batch(B - 1, last=True)
            for j in range(GROUP):
                rank_part(B - 1, 1, j)
            turn = turn_no(B - 1) + KT
            final(B - 2, turn)
            final(B - 1, turn + KT)

        @block.tensor
        def _(pe):
            pe.wait_ge(constants, 3)

            def turn_back(src):
                for n in range(KT):
                    for t in range(2):
                        for k in range(KT):
                            mm = pe.transpose(turn_ps[n][:, t * D + k * P:t * D + (k + 1) * P],
                                              src[:, k, (2 * n + t) * P:(2 * n + t + 1) * P], ident[:, :])
                    mm.then_inc(turned, 1)

            def turn_attn(b):
                pe.wait_ge(attn_loaded, 16 * b)
                turn_back(attn_in)

            def turn_y(b):
                pe.wait_ge(y_scaled, KT * b + KT)
                turn_back(y_T)

            def turn_h(b):
                pe.wait_ge(x1_ready, KT * b)
                pe.wait_ge(x1_normed, TT * b)
                for k in range(KT):
                    for t in range(TT):
                        mm = pe.transpose(turn_ps[k][:, t * P:(t + 1) * P], x1_hat[:, t, k * P:(k + 1) * P], ident[:, :])
                    mm.then_inc(turned, 1)

            def gate_up(b, c, j, reused=True):
                if reused:
                    pe.wait_ge(hid_ready, unit_no(b, c, j) - 1)
                cols = slice((c * GROUP + j) * P, (c * GROUP + j + 1) * P)
                for m, (w, bank) in enumerate(((wg, gate_ps[j % 2]), (wu, up_ps[j % 2]))):
                    for k in range(KT):
                        if c == 0 and j == 0 and m == 0 and not (isinstance(b, int) and b == 0):
                            pe.wait_ge(h2_ready, KT * (b - 1) + k + 1)
                        for n, (l, r) in enumerate(split_passes(w[0][:, k, cols], w[1][:, k, cols],
                                                                h2T[0][:, k, :], h2T[1][:, k, :])):
                            mm = pe.matmul(bank[:, :], l, r, start=(k == 0 and n == 0), stop=(k == KT - 1 and n == 2))
                mm.then_inc(unit_done, 1)

            def down(b, c, j, free=True):
                if c == 0 and j == 0 and free:
                    pe.wait_ge(y_scaled, KT * b)
                pe.wait_ge(kept_ready, unit_no(b, c, j) + 1)
                for k in range(KT):
                    cols = slice(k * P, (k + 1) * P)
                    t = c * GROUP + j
                    for n, (l, r) in enumerate(split_passes(wd[0][:, t, cols], wd[1][:, t, cols],
                                                            kept[c][0][:, j, :], kept[c][1][:, j, :])):
                        mm = pe.matmul(down_ps[k][:, :], l, r, start=(t == 0 and n == 0),
                                       stop=(t == UNITS - 1 and n == 2))
                if t == UNITS - 1:
                    mm.then_inc(down_summed, 1)

            def batch(b, first=False, last=False, y=True, down_free=True):
                for j in range(GROUP):
                    gate_up(b, 0, j, reused=not (first and j < 2))
                    if j > 0 and not first:
                        down(b - 1, 0, j - 1, down_free)
                    if j == 0 and y:
                        pe.wait_ge(h2_full_ready, KT * b)
                        turn_y(b - 2)
                    if j == (1 if first else 2) and not last:
                        if y:
                            pe.wait_ge(y_ready, KT * (b - 1))
                        elif not first:
                            pe.wait_ge(h2_full_ready, KT * b)
                        turn_attn(b + 1)
                gate_up(b, 1, 0)
                if not first:
                    down(b - 1, 0, 3)
                gate_up(b, 1, 1)
                if not first:
                    down(b - 1, 1, 0)
                gate_up(b, 1, 2)
                if not first:
                    down(b - 1, 1, 1)
                if not last:
                    turn_h(b + 1)
                gate_up(b, 1, 3)
                if not first:
                    down(b - 1, 1, 2)
                    down(b - 1, 1, 3)

            batch(0, first=True, y=False)
            pe.wait_ge(down_weights_ready, 2)
            batch(1, y=False, down_free=False)
            batch(2)
            with pe.Fori(3, B - 1) as b:
                batch(b)
            batch(B - 1, last=True)
            for c in range(CT):
                for j in range(GROUP):
                    down(B - 1, c, j)
                    if c == 0 and j == 1:
                        pe.wait_ge(y_ready, KT * (B - 2))
                        turn_y(B - 2)
            pe.wait_ge(y_ready, KT * (B - 1))
            turn_y(B - 1)


def build(nc, x, wqT, wkT, wvT, woT, wg, wu, wd, cT, wmod, out):
    attn_T = nc.dram_tensor("attn_T", (B, D, S), F32, kind="Internal").ap()
    with ExitStack() as ctx:
        def sb(name, shape, dt):
            return ctx.enter_context(nc.sbuf_tensor(name, shape, dt))

        mods = sb("mods", [P, 12, B], F32)
        shared = {
            "x1_first": sb("x1_first", [P, TT, D], F32),
            "wv_gate_up": [sb(f"wv_gate_up_{s}", [P, KT, HD], F32R) for s in ("hi", "lo")],
            "hT": [sb(f"hT_{s}", [P, KT, S], F32R) for s in ("hi", "lo")],
            "xin": sb("xin", [P, TT, D], F32),
            "h_full": sb("h_full", [P, KT, S], F32),
            "out_T": sb("out_T", [P, KT, S], F32),
            "out_T_free": ctx.enter_context(nc.semaphore("out_T_free")),
        }
        attention_phase(nc, x, cT, wmod, wqT, wkT, wvT, woT, wg, wu, attn_T, mods, shared)
        mlp_phase(nc, x, attn_T, wd, out, mods, shared)


def kernel(**inputs):
    import concourse.bacc as bacc
    from concourse.bass_utils import run_bass_kernel_spmd as run

    def by_partition(w):
        t = w.shape[0] // P
        return w.reshape(t, P, w.shape[1]).transpose(1, 0, 2).reshape(P, t * w.shape[1])

    def grouped(w):
        return w.reshape(w.shape[0], CT, P, GROUP).transpose(0, 1, 3, 2).reshape(w.shape[0], I)

    a = {k: np.asarray(val) for k, val in inputs.items()}
    wd = a["L0_ffn_w_down"].reshape(CT, P, GROUP, D).transpose(1, 0, 2, 3).reshape(P, CT * GROUP * D)
    arrays = {
        "x": a["L0_attn_resid_pre"],
        "wqT": by_partition(a["L0_attn_Wq"].T),
        "wkT": by_partition(a["L0_attn_Wk"].T),
        "wvT": by_partition(a["L0_attn_Wv"].T),
        "woT": by_partition(a["L0_attn_Wo"].T),
        "wg": by_partition(grouped(a["L0_ffn_w_gate"])),
        "wu": by_partition(grouped(a["L0_ffn_w_up"])),
        "wd": wd,
        "cT": a["L0_c"].T.reshape(KT, P, B).transpose(1, 0, 2),
        "wmod": a["L0_wmod"].reshape(KT, P, 6 * D).transpose(1, 0, 2),
    }
    arrays = {k: np.ascontiguousarray(val) for k, val in arrays.items()}
    nc = bacc.Bacc("TRN2", target_bir_lowering=False, num_devices=1)
    args = [nc.dram_tensor(k, val.shape, F32, kind="ExternalInput").ap() for k, val in arrays.items()]
    out = nc.dram_tensor("out", (B, S, D), F32, kind="ExternalOutput").ap()
    build(nc, *args, out)
    r = run(nc, [arrays], core_ids=[0])
    return r.results[0]["out"]
```
